# Optimizing a Trainium2 kernel written in Bass

```python
import numpy as np
import jax
import jax.numpy as jnp

def _softmax(x, axis=-1):
    return jax.nn.softmax(x, axis=axis)

def _gelu(x):
    return jax.nn.gelu(x, approximate=True)

def _silu(x):
    return jax.nn.silu(x)

def _sigmoid(x):
    return jax.nn.sigmoid(x)

def _layernorm(x, axis=-1, eps=1e-05):
    m = jnp.mean(x, axis=axis, keepdims=True)
    v = jnp.var(x, axis=axis, keepdims=True)
    return (x - m) / jnp.sqrt(v + eps)

def _scatter_add(tgt, idx, src, axis=0):
    return tgt.at[idx].add(src)

def _segment_sum(src, seg, n):
    return jax.ops.segment_sum(src, seg, n)
kernel_name = 'mk_cond_seq_d2_seqx_r4_c2bbf0'

def setup_inputs(seed: int=0):
    np.random.seed(seed)
    _w = jnp.asarray

    def _rec_inputs():
        import jax
        import jax.numpy as jnp
        _rk = jax.random.key(seed)
        x = -0.000125 + 0.9999 * jax.random.normal(jax.random.fold_in(_rk, 1), (4, 512, 256), jnp.float32)
        _lenS = 512 - jax.random.randint(jax.random.fold_in(_rk, 7), (4,), 0, max(1, 512 // 4) + 1, jnp.int32)
        _lenS2 = 512 - jax.random.randint(jax.random.fold_in(_rk, 8), (4,), 0, max(1, 512 // 4) + 1, jnp.int32)
        cond_256 = 0.0061147 + 1.02565 * jax.random.normal(jax.random.fold_in(_rk, 11), (4, 64), jnp.float32)
        return (x, cond_256)
    x, cond_256 = _rec_inputs()

    def _L0_cond_setup():
        import jax, jax.numpy as jnp
        import numpy as np
        DIM = 256
        BN = 128
        H = 64
        DELTA_SCALE = 0.1
        key = jax.random.key(seed)
        ks = jax.random.split(key, 10)
        B, L = (16, 512)

        def init(k, shape, fan_in):
            bound = 1.0 / np.sqrt(fan_in)
            return jax.random.uniform(k, shape, jnp.float32, -bound, bound)
        return {'x': jax.random.normal(ks[0], (B, L, DIM), jnp.float32), 'h_lang': jax.random.normal(ks[1], (B, H), jnp.float32), 'Wd': init(ks[2], (BN, DIM), DIM), 'bd': init(ks[3], (BN,), DIM), 'Wu': init(ks[4], (DIM, BN), BN), 'bu': init(ks[5], (DIM,), BN), 'Wdd': init(ks[6], (BN * DIM, H), H), 'bdd': init(ks[7], (BN * DIM,), H), 'Wdu': init(ks[8], (DIM * BN, H), H), 'bdu': init(ks[9], (DIM * BN,), H)}
    _L0_cond_all = _L0_cond_setup()
    _L0_cond_in = {k: v for k, v in _L0_cond_all.items() if k in ('Wd', 'bd', 'Wu', 'bu', 'Wdd', 'bdd', 'Wdu', 'bdu')}
    del _L0_cond_all

    def _L1_cond_setup():
        import jax, jax.numpy as jnp
        import numpy as np
        from math import sqrt
        D_MODEL = 256
        N_HEADS = 16
        D_T = 64
        D_HID = 4 * D_MODEL
        EPS = 1e-06

        def _rmsnorm(x):
            return x * jax.lax.rsqrt(jnp.mean(x * x, axis=-1, keepdims=True) + EPS)

        def _ada_rmsnorm(x, t, gamma_w, beta_w):
            gamma = (t @ gamma_w.T)[:, None, :]
            beta = (t @ beta_w.T)[:, None, :]
            return gamma * _rmsnorm(x) + beta

        def _attention(x, W_q, W_k, W_v, W_o):
            b, l, dm = x.shape
            d_head = dm // N_HEADS
            scale = sqrt(N_HEADS / dm)

            def split(y):
                return y.reshape(b, l, N_HEADS, d_head).transpose(0, 2, 1, 3)
            q = split(x @ W_q.T)
            k = split(x @ W_k.T)
            v = split(x @ W_v.T)
            attn = jax.nn.softmax(scale * jnp.einsum('bnqd,bnkd->bnqk', q, k), axis=-1)
            o = jnp.einsum('bnqk,bnkd->bnqd', attn, v)
            o = o.transpose(0, 2, 1, 3).reshape(b, l, dm)
            return o @ W_o.T

        def _swiglu(x, gate_w, hidden_w, out_w, out_b):
            return jax.nn.silu(x @ gate_w.T) * (x @ hidden_w.T) @ out_w.T + out_b
        key = jax.random.key(seed)
        ks = jax.random.split(key, 16)
        s = 0.02
        inp = {'x': jax.random.normal(ks[0], (4, 512, D_MODEL), dtype=jnp.float32), 't': jax.random.normal(ks[1], (4, D_T), dtype=jnp.float32), 'attn_gamma_w': jax.random.normal(ks[2], (D_MODEL, D_T), dtype=jnp.float32) * s, 'attn_beta_w': jax.random.normal(ks[3], (D_MODEL, D_T), dtype=jnp.float32) * s, 'W_q': jax.random.normal(ks[4], (D_MODEL, D_MODEL), dtype=jnp.float32) * s, 'W_k': jax.random.normal(ks[5], (D_MODEL, D_MODEL), dtype=jnp.float32) * s, 'W_v': jax.random.normal(ks[6], (D_MODEL, D_MODEL), dtype=jnp.float32) * s, 'W_o': jax.random.normal(ks[7], (D_MODEL, D_MODEL), dtype=jnp.float32) * s, 'attn_alpha_w': jax.random.normal(ks[8], (D_MODEL, D_T), dtype=jnp.float32) * s, 'ffn_gamma_w': jax.random.normal(ks[9], (D_MODEL, D_T), dtype=jnp.float32) * s, 'ffn_beta_w': jax.random.normal(ks[10], (D_MODEL, D_T), dtype=jnp.float32) * s, 'gate_w': jax.random.normal(ks[11], (D_HID, D_MODEL), dtype=jnp.float32) * s, 'hidden_w': jax.random.normal(ks[12], (D_HID, D_MODEL), dtype=jnp.float32) * s, 'out_w': jax.random.normal(ks[13], (D_MODEL, D_HID), dtype=jnp.float32) * s, 'out_b': jnp.zeros((D_MODEL,), dtype=jnp.float32), 'ffn_alpha_w': jax.random.normal(ks[14], (D_MODEL, D_T), dtype=jnp.float32) * s}
        return inp
    _L1_cond_all = _L1_cond_setup()
    _L1_cond_in = {k: v for k, v in _L1_cond_all.items() if k in ('attn_gamma_w', 'attn_beta_w', 'W_q', 'W_k', 'W_v', 'W_o', 'attn_alpha_w', 'ffn_gamma_w', 'ffn_beta_w', 'gate_w', 'hidden_w', 'out_w', 'out_b', 'ffn_alpha_w')}
    del _L1_cond_all
    return {'x': x, 'cond_256': cond_256, 'L0_cond_Wd': _L0_cond_in['Wd'], 'L0_cond_bd': _L0_cond_in['bd'], 'L0_cond_Wu': _L0_cond_in['Wu'], 'L0_cond_bu': _L0_cond_in['bu'], 'L0_cond_Wdd': _L0_cond_in['Wdd'], 'L0_cond_bdd': _L0_cond_in['bdd'], 'L0_cond_Wdu': _L0_cond_in['Wdu'], 'L0_cond_bdu': _L0_cond_in['bdu'], 'L1_cond_attn_gamma_w': _L1_cond_in['attn_gamma_w'], 'L1_cond_attn_beta_w': _L1_cond_in['attn_beta_w'], 'L1_cond_W_q': _L1_cond_in['W_q'], 'L1_cond_W_k': _L1_cond_in['W_k'], 'L1_cond_W_v': _L1_cond_in['W_v'], 'L1_cond_W_o': _L1_cond_in['W_o'], 'L1_cond_attn_alpha_w': _L1_cond_in['attn_alpha_w'], 'L1_cond_ffn_gamma_w': _L1_cond_in['ffn_gamma_w'], 'L1_cond_ffn_beta_w': _L1_cond_in['ffn_beta_w'], 'L1_cond_gate_w': _L1_cond_in['gate_w'], 'L1_cond_hidden_w': _L1_cond_in['hidden_w'], 'L1_cond_out_w': _L1_cond_in['out_w'], 'L1_cond_out_b': _L1_cond_in['out_b'], 'L1_cond_ffn_alpha_w': _L1_cond_in['ffn_alpha_w']}

def reference(x, cond_256, L0_cond_Wd, L0_cond_bd, L0_cond_Wu, L0_cond_bu, L0_cond_Wdd, L0_cond_bdd, L0_cond_Wdu, L0_cond_bdu, L1_cond_attn_gamma_w, L1_cond_attn_beta_w, L1_cond_W_q, L1_cond_W_k, L1_cond_W_v, L1_cond_W_o, L1_cond_attn_alpha_w, L1_cond_ffn_gamma_w, L1_cond_ffn_beta_w, L1_cond_gate_w, L1_cond_hidden_w, L1_cond_out_w, L1_cond_out_b, L1_cond_ffn_alpha_w):
    import jax
    import jax.numpy as jnp

    def _L0_cond_ref(x, h_lang, Wd, bd, Wu, bu, Wdd, bdd, Wdu, bdu):
        import jax, jax.numpy as jnp
        import numpy as np
        DIM = 256
        BN = 128
        H = 64
        DELTA_SCALE = 0.1
        B, L, D = x.shape
        dWd = ((h_lang @ Wdd.T + bdd) * DELTA_SCALE).reshape(B, BN, D)
        dWu = ((h_lang @ Wdu.T + bdu) * DELTA_SCALE).reshape(B, D, BN)
        Wd_b = Wd + dWd
        Wu_b = Wu + dWu
        down = jax.nn.relu(jnp.einsum('bld,bnd->bln', x, Wd_b) + bd)
        up = jnp.einsum('bln,bdn->bld', down, Wu_b) + bu
        return x + up

    def _L1_cond_ref(x, t, attn_gamma_w, attn_beta_w, W_q, W_k, W_v, W_o, attn_alpha_w, ffn_gamma_w, ffn_beta_w, gate_w, hidden_w, out_w, out_b, ffn_alpha_w):
        import jax, jax.numpy as jnp
        import numpy as np
        from math import sqrt
        D_MODEL = 256
        N_HEADS = 16
        D_T = 64
        D_HID = 4 * D_MODEL
        EPS = 1e-06

        def _rmsnorm(x):
            return x * jax.lax.rsqrt(jnp.mean(x * x, axis=-1, keepdims=True) + EPS)

        def _ada_rmsnorm(x, t, gamma_w, beta_w):
            gamma = (t @ gamma_w.T)[:, None, :]
            beta = (t @ beta_w.T)[:, None, :]
            return gamma * _rmsnorm(x) + beta

        def _attention(x, W_q, W_k, W_v, W_o):
            b, l, dm = x.shape
            d_head = dm // N_HEADS
            scale = sqrt(N_HEADS / dm)

            def split(y):
                return y.reshape(b, l, N_HEADS, d_head).transpose(0, 2, 1, 3)
            q = split(x @ W_q.T)
            k = split(x @ W_k.T)
            v = split(x @ W_v.T)
            attn = jax.nn.softmax(scale * jnp.einsum('bnqd,bnkd->bnqk', q, k), axis=-1)
            o = jnp.einsum('bnqk,bnkd->bnqd', attn, v)
            o = o.transpose(0, 2, 1, 3).reshape(b, l, dm)
            return o @ W_o.T

        def _swiglu(x, gate_w, hidden_w, out_w, out_b):
            return jax.nn.silu(x @ gate_w.T) * (x @ hidden_w.T) @ out_w.T + out_b
        a_alpha = (t @ attn_alpha_w.T)[:, None, :]
        x = x + a_alpha * _attention(_ada_rmsnorm(x, t, attn_gamma_w, attn_beta_w), W_q, W_k, W_v, W_o)
        f_alpha = (t @ ffn_alpha_w.T)[:, None, :]
        return x + f_alpha * _swiglu(_ada_rmsnorm(x, t, ffn_gamma_w, ffn_beta_w), gate_w, hidden_w, out_w, out_b)
    x = _L0_cond_ref(x, cond_256, L0_cond_Wd, L0_cond_bd, L0_cond_Wu, L0_cond_bu, L0_cond_Wdd, L0_cond_bdd, L0_cond_Wdu, L0_cond_bdu)
    x = _L1_cond_ref(x, cond_256, L1_cond_attn_gamma_w, L1_cond_attn_beta_w, L1_cond_W_q, L1_cond_W_k, L1_cond_W_v, L1_cond_W_o, L1_cond_attn_alpha_w, L1_cond_ffn_gamma_w, L1_cond_ffn_beta_w, L1_cond_gate_w, L1_cond_hidden_w, L1_cond_out_w, L1_cond_out_b, L1_cond_ffn_alpha_w)
    return x

_drawn_inputs = setup_inputs


def setup_inputs(seed=0):
    import zlib

    import numpy as np

    out = dict(_drawn_inputs(seed))
    spreads = {'L1_cond_out_b': (0.0, 0.625)}
    factors = {'L0_cond_bd': 3.107,
     'L1_cond_attn_gamma_w': 8.0,
     'L1_cond_attn_beta_w': 8.0,
     'L1_cond_W_q': 8.0,
     'L1_cond_W_k': 8.0,
     'L1_cond_W_v': 8.0,
     'L1_cond_W_o': 8.0,
     'L1_cond_attn_alpha_w': 8.0,
     'L1_cond_ffn_gamma_w': 8.0,
     'L1_cond_ffn_beta_w': 8.0,
     'L1_cond_gate_w': 8.0,
     'L1_cond_hidden_w': 8.0,
     'L1_cond_out_w': 8.0,
     'L1_cond_ffn_alpha_w': 4.568}
    for name, (base, spread) in spreads.items():
        noise = np.random.default_rng([zlib.crc32(name.encode()), seed]).standard_normal(out[name].shape)
        drawn = base * np.exp(spread * noise) if base else spread * noise
        out[name] = jnp.asarray(drawn.astype(out[name].dtype))
    for name, factor in factors.items():
        out[name] = (out[name] * factor).astype(out[name].dtype)
    return out
```

```python
import numpy as np
import concourse.bass as bass
from concourse import mybir
from contextlib import ExitStack

F32, F32R = mybir.dt.float32, mybir.dt.float32r
ALU = mybir.AluOpType
ACT = mybir.ActivationFunctionType
AX_X = mybir.AxisListType.X

P = 128
EPS = 1e-6
DELTA = 0.1
GATED_HI_LO = ((0, 0), (1, 0), (0, 1))


def adapter_block_kernel(nc, x, cond, Wd, bd, Wu, bu, Wdd, bdd, Wdu, bdu, cond_ws, Wq, Wk, Wv, Wo,
                         gate_w, hidden_w, out_w, out_b, out):
    B, L, D = x.shape
    BN = Wd.shape[0]
    HC = cond.shape[1]
    DH = 16
    NH = D // DH
    F = gate_w.shape[0]
    DC = D // P
    FC = F // P
    NT = L // P
    G = NH // 4
    HH = NH // DC
    SCALE = (NH / D) ** 0.5
    assert BN == P and HC == 64 and L == 512 and DC == 2 and NT == 4 and G == 4

    with ExitStack() as ctx:
        def sem(name):
            return ctx.enter_context(nc.semaphore(name))

        end_of = [16512]

        def place(name, shape, dt=F32, at=None):
            size = 4 * int(np.prod(shape[1:]))
            start = end_of[0] if at is None else at
            if at is None:
                end_of[0] = -(-(start + size) // 32) * 32
            assert start + size <= 229344, (name, start + size)
            return nc.alloc_sbuf_tensor_at(name, shape, dt, offset=start)

        ps = ctx.enter_context(nc.psum_tensor("ps", [P, 8, 512], F32))
        dw_scr = nc.dram_tensor("dw_scr", (2, 8, 2, 64, P), F32).ap()
        qk_scr = nc.dram_tensor("qk_scr", (2, 2, D, L), F32).ap()

        ident = place("ident", [P, P])
        ones = place("ones", [P, P])
        epsc = place("epsc", [P, 1])
        bdc = place("bdc", [P, 1])
        buc = place("buc", [P, DC])
        obc = place("obc", [P, DC])
        conds = place("conds", [P, 6, 8])
        base = place("base", [P, 512])
        wqk = place("wqk", [P, 2, 2, DC, D], F32R)
        wv = place("wv", [P, DC, D])
        wo = place("wo", [P, 2, G, D], F32R)
        gw = place("gw", [P, 2, DC, F], F32R)
        hw = place("hw", [P, 2, DC, F], F32R)
        ow = place("ow", [P, 2, FC, D], F32R)
        loop_base = end_of[0]

        NST = 4
        dd_in = place("dd_in", [P, NST, 2048])
        ddT = place("ddT", [P, 2, 4, 512])
        dw_out = place("dw_out", [P, 2, 4, 512])
        qkvo_in = place("qkvo_in", [P, 4, DC, D])
        wo_pad = place("wo_pad", [P, DC, G, 4, 32])
        gh_in = place("gh_in", [P, 2, FC, D])
        ow_in = place("ow_in", [P, DC, F])
        base_in = place("base_in", [P, 512])
        bias_in = place("bias_in", [P, 512])
        cw_in = place("cw_in", [P, 6, 2, HC])
        cwT = place("cwT", [P, 6, P])
        csel = place("csel", [P, 32])

        end_of[0] = loop_base
        kst = place("kst", [P, HH, L], F32R)
        qst = place("qst", [P, HH, L], F32R)
        NPR = 3
        probs_at = end_of[0]
        probs = place("probs", [P, NPR, 4, L])
        vaug = place("vaug", [P, NT, NH, 32])
        xnat = place("xnat", [P, NT, D])
        xr = place("xr", [P, DC, L])
        xs = place("xs", [P, 2, DC, L], F32R)
        dn = place("dn", [P, L])
        dns = place("dns", [P, 2, L], F32R)
        xn = place("xn", [P, DC, L])
        rs = place("rs", [P, L])
        dwl = place("dwl", [P, 512])
        wa = place("wa", [P, 2, 512], F32R)
        qkf = place("qkf", [P, DC, L])
        qks = place("qks", [P, 2, DC, L], F32R)
        negmax = place("negmax", [P, NH, NT])
        negrow = place("negrow", [16, G, P], F32R)
        u = place("u", [P, L])
        den = place("den", [P, L])
        xb = place("xb", [P, DC, L])
        os_at = end_of[0]
        os_ = place("os_", [P, 2, G, L], F32R)
        act = place("act", [P, 2, L], at=os_at)
        acts = place("acts", [P, 2, 2, L], F32R, at=os_at + 4096)
        ys = place("ys", [P, 2, DC, L], F32R, at=probs_at)
        yn = place("yn", [P, DC, L], at=probs_at + 8192)
        onat = place("onat", [P, NT, D], at=probs_at + 12288)
        rsb = place("rsb", [P, L], at=probs_at + 16384)
        sg = place("sg", [P, L], at=probs_at + 18432)
        tmp = place("tmp", [P, L], at=probs_at + 20480)

        groups = ["cond0", "cond1", "condm", "base", "q", "k", "v", "o0", "o1"]
        groups += [f"{w}{k}{half}" for w in "gh" for k in range(DC) for half in range(2)]
        groups += [f"w{p}" for p in range(FC // 2)]
        loads_of = {"cond0": "cw", "cond1": "cw", "condm": "cond", "base": "base"}
        NCH = 16
        first_group = [-(-c * len(groups) // NCH) for c in range(NCH + 1)]

        dd_loaded = sem("dd_loaded")
        dd_loaded = [dd_loaded] + [sem(f"dd_loaded{i}") for i in range(1, NST)]
        w_loaded = {n: sem(f"w_loaded_{n}") for n in ("cond", "cw", "base", "qkvo", "gate", "hidden", "outw", "vec")}
        const_ready = sem("const_ready")
        base_summed = sem("base_summed")
        pad_ready = sem("pad_ready")
        ddT_ready = sem("ddT_ready")
        ddT_copied_a = sem("ddT_copied_a")
        ddT_copied_v = sem("ddT_copied_v")
        dw_ready = sem("dw_ready")
        dw_copied = sem("dw_copied")
        dw_stored = [sem("dw_stored0"), sem("dw_stored1")]
        wt_ready = sem("wt_ready")
        wt_hi = sem("wt_hi")
        wt_copied = sem("wt_copied")
        cwT_copied = sem("cwT_copied")
        stack_zeroed = sem("stack_zeroed")
        stack_ones = sem("stack_ones")
        vones = sem("vones")

        def blocks_of(g):
            if g == "cond0":
                return [(cw_in[:, k, :, :].rearrange("p e h -> p (e h)"), k * P) for k in range(4)]
            if g == "cond1":
                return [(cw_in[:, k, :, :].rearrange("p e h -> p (e h)"), (k - 4) * P) for k in range(4, 6)]
            if g == "base":
                return [(base_in[:, i * P:(i + 1) * P], i * P) for i in range(4)]
            if g in "qkv":
                i = "qkv".index(g)
                return [(qkvo_in[:, i, m, k * P:(k + 1) * P], k * D + m * P) for k in range(DC) for m in range(DC)]
            if g[0] == "o":
                return [(wo_pad[:, m, 2 * int(g[1]) + i, :, :].rearrange("p j r -> p (j r)"), i * D + m * P)
                        for i in range(2) for m in range(DC)]
            if g[0] in "gh":
                w, k, half = "gh".index(g[0]), int(g[1]), int(g[2])
                return [(gh_in[:, w, 4 * half + i, k * P:(k + 1) * P], i * P) for i in range(4)]
            p = int(g[1])
            return [(ow_in[:, m, (2 * p + i) * P:(2 * p + i + 1) * P], i * D + m * P)
                    for i in range(2) for m in range(DC)]

        def kept_at(g, part):
            if g in "qk":
                return wqk[:, "qk".index(g), part, :, :].rearrange("p k n -> p (k n)")
            if g[0] == "o":
                i = 2 * int(g[1])
                return wo[:, part, i:i + 2, :].rearrange("p g n -> p (g n)")
            if g[0] in "gh":
                k, half = int(g[1]), int(g[2])
                return (gw if g[0] == "g" else hw)[:, part, k, half * 512:(half + 1) * 512]
            p = int(g[1])
            return ow[:, part, 2 * p:2 * p + 2, :].rearrange("p f n -> p (f n)")

        def load_name(g):
            if g in loads_of:
                return loads_of[g]
            return {"q": "qkvo", "k": "qkvo", "v": "qkvo", "o": "qkvo", "g": "gate", "h": "hidden", "w": "outw"}[g[0]]

        with nc.Block() as block:
            @block.sync
            def _(sp):
                for e in range(2):
                    for b in range(B):
                        if e == 0 and b == 0:
                            sp.wait_ge(const_ready, 1)
                        col = cond[b:b + 1, :].rearrange("b h -> h b")
                        sp.dma_start(csel[e * HC:(e + 1) * HC, 2 * b + e:2 * b + e + 1], col).then_inc(w_loaded["cond"], 16)
                for k, w in enumerate(cond_ws):
                    sp.dma_start(cw_in[:, k], w.rearrange("(e p) h -> p e h", p=P)).then_inc(w_loaded["cw"], 16)

                def chunk(c):
                    if c >= NST:
                        sp.wait_ge(ddT_ready, 4 * (c - NST + 1))
                    if c < NCH // 2:
                        src = Wdd.rearrange("(n d) h -> n (d h)", d=D)[:, c * 2048:(c + 1) * 2048]
                    else:
                        dc, nb = divmod(c - NCH // 2, 4)
                        src = Wdu.rearrange("(dc dp n) h -> dc dp (n h)", dc=DC, n=BN)[dc][:, nb * 2048:(nb + 1) * 2048]
                    sp.dma_start(dd_in[:, c % NST], src).then_inc(dd_loaded[c % NST], 16)

                chunk(0)
                sp.dma_start(base_in[:, 0:D], Wd).then_inc(w_loaded["base"], 16)
                sp.dma_start(base_in[:, D:512], Wu.rearrange("(c p) n -> p c n", p=P)).then_inc(w_loaded["base"], 16)
                sp.dma_start(bias_in[:, 0:D], bdd.rearrange("(n d) -> n d", d=D)).then_inc(w_loaded["base"], 16)
                sp.dma_start(bias_in[:, D:512], bdu.rearrange("(c p n) -> p c n", p=P, n=BN)).then_inc(w_loaded["base"], 16)
                chunk(1)
                for i, w in enumerate((Wq, Wk, Wv, Wo)):
                    sp.dma_start(qkvo_in[:, i], w.rearrange("(m p) k -> p m k", p=P)).then_inc(w_loaded["qkvo"], 16)
                chunk(2)
                sp.dma_start(gh_in[:, 0], gate_w.rearrange("(f p) k -> p f k", p=P)).then_inc(w_loaded["gate"], 16)
                chunk(3)
                sp.dma_start(gh_in[:, 1], hidden_w.rearrange("(f p) k -> p f k", p=P)).then_inc(w_loaded["hidden"], 16)
                sp.dma_start(ow_in[:], out_w.rearrange("(m p) f -> p m f", p=P)).then_inc(w_loaded["outw"], 16)
                sp.dma_start(bdc[:], bd.rearrange("(p o) -> p o", o=1)).then_inc(w_loaded["vec"], 16)
                for c in range(DC):
                    for to, vec in ((buc, bu), (obc, out_b)):
                        src = vec[c * P:(c + 1) * P].rearrange("(p o) -> p o", o=1)
                        sp.dma_start(to[:, c:c + 1], src).then_inc(w_loaded["vec"], 16)
                for c in range(4, NCH):
                    chunk(c)
                sp.wait_ge(w_loaded["vec"], 80)

            @block.gpsimd
            def _(pool):
                nc.gpsimd.memset(csel[:], 0.0).then_inc(const_ready, 1)
                nc.gpsimd.memset(ident[:], 0.0).then_inc(const_ready, 1)
                nc.gpsimd.memset(ones[:], 1.0).then_inc(const_ready, 1)
                nc.gpsimd.memset(epsc[:], EPS).then_inc(const_ready, 1)
                pool.wait_ge(const_ready, 4)
                nc.gpsimd.affine_select(out=ident[:], in_=ident[:], compare_op=ALU.not_equal, fill=1.0, base=0,
                                        pattern=[[-1, P]], channel_multiplier=1).then_inc(const_ready, 1)
                nc.gpsimd.memset(wo_pad[:], 0.0).then_inc(pad_ready, 1)
                pool.wait_ge(w_loaded["base"], 64)
                nc.gpsimd.tensor_scalar(bias_in[:], bias_in[:], DELTA, None, ALU.mult).then_inc(base_summed, 1)
                pool.wait_ge(base_summed, 1)
                nc.gpsimd.tensor_tensor(base_in[:], base_in[:], bias_in[:], ALU.add).then_inc(base_summed, 1)
                pool.wait_ge(w_loaded["qkvo"], 64)
                pool.wait_ge(pad_ready, 1)
                for m in range(DC):
                    nc.gpsimd.tensor_copy(wo_pad[:, m, :, :, 0:DH],
                                          qkvo_in[:, 3, m, :].rearrange("p (g j r) -> p g j r", g=G, j=4)).then_inc(pad_ready, 1)
                for r in range(4):
                    pool.wait_ge(dw_copied, 4 * (r + 1))
                    for g in range(4):
                        dst = dw_scr[r // 2, :, r % 2].rearrange("p (c g j) n -> g p c (j n)", c=4, g=4)[g]
                        pool.dma_start(dst, dw_out[32 * g:32 * g + 8, r % 2]).then_inc(dw_stored[r % 2], 16)
                for s in dw_stored:
                    pool.wait_ge(s, 128)

            @block.tensor
            def _(pe):
                def dd_transposes(c):
                    pe.wait_ge(dd_loaded[c % NST], 16 * (c // NST + 1))
                    for t in range(4):
                        if c >= 1:
                            pe.wait_ge(ddT_copied_v if t < 2 else ddT_copied_a, 2 * (c - 1) + t % 2 + 1)
                        for i in range(4):
                            j = 4 * t + i
                            mm = pe.transpose(ps[:, t, i * P:(i + 1) * P], dd_in[:, c % NST, j * P:(j + 1) * P], ident[:])
                        mm.then_inc(ddT_ready, 1)

                def dd_products(c):
                    pe.wait_ge(ddT_copied_v, 2 * (c + 1))
                    pe.wait_ge(ddT_copied_a, 2 * (c + 1))
                    if c >= 2:
                        pe.wait_ge(dw_copied, c - 1)
                    for t in range(4):
                        mm = pe.matmul(ps[32 * t:32 * t + 32, 4 + c % 2, :], csel[:], ddT[:, c % 2, t, :], start=True, stop=True)
                    mm.then_inc(dw_ready, 1)

                def weights(i):
                    g = groups[i]
                    if g == "condm":
                        pe.wait_ge(cwT_copied, 2)
                        pe.wait_ge(w_loaded["cond"], 128)
                        if i >= 2:
                            pe.wait_ge(wt_copied, i - 1)
                        for k in range(6):
                            mm = pe.matmul(ps[:, 6 + i % 2, 32 * k:32 * k + 32], cwT[:, k, :], csel[:], start=True, stop=True)
                        mm.then_inc(wt_ready, 1)
                        return
                    if g == "base":
                        pe.wait_ge(base_summed, 2)
                    elif g[0] == "o":
                        pe.wait_ge(pad_ready, 1 + DC)
                    else:
                        pe.wait_ge(w_loaded[load_name(g)], {"cw": 96, "qkvo": 64}.get(load_name(g), 16))
                    if i >= 2:
                        pe.wait_ge(wt_copied, i - 1)
                    for src, col in blocks_of(g):
                        mm = pe.transpose(ps[:, 6 + i % 2, col:col + P], src, ident[:])
                    mm.then_inc(wt_ready, 1)

                pe.wait_ge(const_ready, 5)
                for c in range(NCH):
                    if c == 1:
                        pe.wait_ge(w_loaded["cond"], 128)
                    dd_transposes(c)
                    for i in range(first_group[c], first_group[c + 1]):
                        weights(i)
                    if c >= 1:
                        dd_products(c - 1)
                dd_products(NCH - 1)

            @block.scalar
            def _(act_):
                for c in range(NCH + 1):
                    if c < NCH:
                        if c >= 2:
                            act_.wait_ge(dw_ready, c - 1)
                        for t in (2, 3):
                            act_.wait_ge(ddT_ready, 4 * c + t + 1)
                            nc.scalar.copy(ddT[:, c % 2, t, :], ps[:, t, :]).then_inc(ddT_copied_a, 1)
                    if c >= 1:
                        act_.wait_ge(dw_ready, c)
                        if c > 8:
                            act_.wait_ge(dw_stored[(c - 1) // 4 % 2], 64)
                        nc.scalar.mul(dw_out[:, (c - 1) // 4 % 2, (c - 1) % 4, :], ps[:, 4 + (c - 1) % 2, :], DELTA).then_inc(dw_copied, 1)

            @block.vector
            def _(dve):
                def copy_weights(i):
                    g, bank = groups[i], 6 + i % 2
                    dve.wait_ge(wt_ready, i + 1)
                    if g == "cond0":
                        nc.vector.tensor_copy(cwT[:, 0:4, :].rearrange("p k n -> p (k n)"), ps[:, bank, :]).then_inc(cwT_copied, 1)
                        dve.wait_ge(cwT_copied, 1)
                        nc.vector.engine_nop().then_inc(wt_copied, 1)
                    elif g == "cond1":
                        nc.vector.tensor_copy(cwT[:, 4:6, :].rearrange("p k n -> p (k n)"), ps[:, bank, 0:2 * P]).then_inc(cwT_copied, 1)
                        dve.wait_ge(cwT_copied, 2)
                        nc.vector.engine_nop().then_inc(wt_copied, 1)
                    elif g == "condm":
                        src = ps[:, bank, 0:192].rearrange("p (k n) -> p k n", k=6)[:, :, 0:8]
                        nc.vector.tensor_copy(conds[:], src).then_inc(wt_copied, 1)
                    elif g == "base":
                        nc.vector.tensor_copy(base[:], ps[:, bank, :]).then_inc(wt_copied, 1)
                    elif g == "v":
                        nc.vector.tensor_copy(wv[:].rearrange("p k n -> p (k n)"), ps[:, bank, :]).then_inc(wt_copied, 1)
                    else:
                        nc.vector.tensor_copy(kept_at(g, 0), ps[:, bank, :]).then_inc(wt_hi, 1)
                        split[0] += 1
                        dve.wait_ge(wt_hi, split[0])
                        nc.vector.tensor_tensor(kept_at(g, 1), ps[:, bank, :], kept_at(g, 0), ALU.subtract).then_inc(wt_copied, 1)

                split = [0]
                for c in range(NCH):
                    if c >= 2:
                        dve.wait_ge(dw_ready, c - 1)
                    for t in (0, 1):
                        dve.wait_ge(ddT_ready, 4 * c + t + 1)
                        nc.vector.tensor_copy(ddT[:, c % 2, t, :], ps[:, t, :]).then_inc(ddT_copied_v, 1)
                    for i in range(first_group[c], first_group[c + 1]):
                        copy_weights(i)

        x_loaded, dw_loaded = sem("x_loaded"), sem("dw_loaded")
        parts_stored = [sem("q_stored"), sem("k_stored")]
        stack_loaded = sem("stack_loaded")
        max_loaded = [sem("max_loaded0"), sem("max_loaded1")]
        out_stored = sem("out_stored")
        passed_v, passed_s = sem("passed_v"), sem("passed_s")
        xT_ready, down_ready, up_ready, sum_ready = sem("xT_ready"), sem("down_ready"), sem("up_ready"), sem("sum_ready")
        q_ready, k_ready, v_ready = sem("q_ready"), sem("k_ready"), sem("v_ready")
        xr_copied, x_hi, x_lo, adapter_w = sem("xr_copied"), sem("x_hi"), sem("x_lo"), sem("adapter_w")
        down_act, down_hi, down_lo = sem("down_act"), sem("down_hi"), sem("down_lo")
        x1_ready, x1_sq, x1_sqsum, x1_root, x1_rs = sem("x1_ready"), sem("x1_sq"), sem("x1_sqsum"), sem("x1_root"), sem("x1_rs")
        xn_scaled, xn_ready, xn_hi, xn_lo = sem("xn_scaled"), sem("xn_ready"), sem("xn_hi"), sem("xn_lo")
        qk_copied, qk_hi, qk_lo, v_copied = sem("qk_copied"), sem("qk_hi"), sem("qk_lo"), sem("v_copied")
        x1_moved = sem("x1_moved")
        max_ready, max_read = sem("max_ready"), sem("max_read")
        score_ready, exp_done, pv_done = sem("score_ready"), sem("exp_done"), sem("pv_done")
        u_copied, den_ready, rden_ready, o_scaled, o_hi, o_lo = (sem("u_copied"), sem("den_ready"), sem("rden_ready"),
                                                                 sem("o_scaled"), sem("o_hi"), sem("o_lo"))
        wo_ready, x2_ready, x2_sq, x2_sqsum, x2_sum = sem("wo_ready"), sem("x2_ready"), sem("x2_sq"), sem("x2_sqsum"), sem("x2_sum")
        x2_root, x2_rs, yn_scaled, yn_ready, y_hi, y_lo = (sem("x2_root"), sem("x2_rs"), sem("yn_scaled"), sem("yn_ready"),
                                                          sem("y_hi"), sem("y_lo"))
        gate_ready, hid_ready, silu_done, act_ready, act_hi, act_lo = (sem("gate_ready"), sem("hid_ready"), sem("silu_done"),
                                                                       sem("act_ready"), sem("act_hi"), sem("act_lo"))
        outc_done, ffn_scaled, x3_ready, outT_ready, out_copied = (sem("outc_done"), sem("ffn_scaled"), sem("x3_ready"),
                                                                   sem("outT_ready"), sem("out_copied"))

        A_GAMMA, A_BETA, A_ALPHA, F_GAMMA, F_BETA, F_ALPHA = range(6)

        def cvec(kind, b, c):
            return conds[:, kind, bass.ds(2 * b + c, 1)]

        LEAD, STEPS = 14, 4 * G
        NENT = 2 * NH + G

        def entries(step):
            units = range(0, LEAD) if step < 0 else range(LEAD + 2 * step, LEAD + 2 * step + 2)
            found = []
            for m in units:
                if m < 2 * NH:
                    found.append(("unit", m))
                if m >= 9 and (m - 9) % 8 == 0 and (m - 9) // 8 < G:
                    found.append(("turn", (m - 9) // 8))
            return found

        number = {}
        for s in range(-1, STEPS):
            for e in entries(s):
                number[e] = len(number)
        assert len(number) == NENT

        FRONT_IN_ATT = {10: ["xT"], 11: ["down"], 12: ["up"], 13: ["sum"], 14: ["norm"]}
        MID = ["out_proj", "qkv", "back_sum", "back_norm", "ffn0", "ffn1", "ffn2", "ffn3", "max", "ffn4", "ffn5", "ffn6", "ffn7",
               "ffn_out", "result"]
        FRONT = ["xT", "down", "up", "sum", "norm", "qkv", "max"]

        def group_of(m):
            return 64 * (m // HH), m % HH

        with nc.Block() as block:
            @block.sync
            def _(sp):
                def load(f, first):
                    if not first:
                        sp.wait_ge(xT_ready, 2 * f)
                        sp.sem_inc(passed_s, 1)
                        sp.wait_ge(adapter_w, 3 * f)
                        sp.sem_inc(passed_s, 1)
                    sp.dma_start(xnat[:], x[bass.ds(f, 1)].rearrange("b (t p) d -> p (b t) d", p=P)).then_inc(x_loaded, 16)
                    for m in range(2):
                        for e in range(2):
                            src = dw_scr[m, bass.ds(2 * f + e, 1)].rearrange("o c r n -> r (o c) n")
                            dst = dwl[e:P:2, m * D:(m + 1) * D].rearrange("p (c n) -> p c n", c=2)
                            sp.dma_start(dst, src).then_inc(dw_loaded, 16)

                def stacks(f, first):
                    for w in range(2):
                        sp.wait_ge(qk_hi, 4 * f + 2 * w + 2)
                        sp.wait_ge(qk_lo, 4 * f + 2 * w + 2)
                        sp.dma_start(qk_scr[w].rearrange("t (c p) l -> p t c l", p=P), qks[:].bitcast(F32)).then_inc(parts_stored[w], 16)
                    if not first:
                        sp.wait_ge(score_ready, 64 * f)
                    for w, stack in ((0, qst), (1, kst)):
                        sp.wait_ge(parts_stored[w], 16 * f + 16)
                        for c in range(DC):
                            for slot in range(3):
                                part = (0, 0, 1)[slot] if w == 0 else (0, 1, 0)[slot]
                                src = qk_scr[w, part, c * P:(c + 1) * P].rearrange("(h d) l -> d h l", d=DH)
                                r0 = 64 * c + DH * slot
                                sp.dma_start(stack[r0:r0 + DH].bitcast(F32), src).then_inc(stack_loaded, 16)

                def max_row(b, g):
                    sp.wait_ge(max_read, NENT * b + number[("turn", g)] + 1)
                    row = 64 * (g // 2) + 48
                    h0 = 4 * (g % 2)
                    sp.dma_start(qst[row:row + 1, h0:h0 + 4, :].bitcast(F32), negrow[:, g, :].bitcast(F32)).then_inc(max_loaded[g % 2], 16)

                def turns(b, step):
                    for kind, g in entries(step):
                        if kind == "turn":
                            max_row(b, g)

                def body(b, more, first=False):
                    for s in range(STEPS):
                        turns(b, s)
                    if more:
                        stacks(b + 1, False)
                        turns(b + 1, -1)
                    sp.wait_ge(out_copied, 2 * b + 2)
                    sp.sem_inc(passed_s, 1)
                    sp.dma_start(out[bass.ds(b, 1)].rearrange("b (t p) d -> p (b t) d", p=P), onat[:]).then_inc(out_stored, 16)

                sp.wait_ge(stack_zeroed, 4)
                for c in range(DC):
                    sp.dma_start(kst[64 * c + 48:64 * c + 49].bitcast(F32), ones[0:32, :]).then_inc(stack_ones, 16)
                sp.wait_ge(stack_ones, 32)
                load(0, True)
                stacks(0, True)
                turns(0, -1)
                load(1, False)
                with sp.Fori(0, B - 2) as b:
                    body(b, True)
                    load(b + 2, False)
                body(B - 2, True)
                body(B - 1, False)
                sp.wait_ge(out_stored, 16 * B)

            @block.tensor
            def _(pe):
                def three_parts(out_, w, d, start, stop):
                    for i, (pw, pd) in enumerate(GATED_HI_LO):
                        mm = pe.matmul(out_, w(pw), d(pd), start=start and i == 0, stop=stop and i == 2)
                    return mm

                def s_xT(f, first):
                    pe.wait_ge(x_loaded, 16 * f + 16)
                    if not first:
                        pe.wait_ge(max_read, NENT * f)
                    for c in range(DC):
                        for t in range(NT):
                            mm = pe.transpose(ps[:, c, t * P:(t + 1) * P], xnat[:, t, c * P:(c + 1) * P], ident[:])
                        mm.then_inc(xT_ready, 1)

                def s_down(f, first):
                    pe.wait_ge(adapter_w, 3 * f + 3)
                    pe.wait_ge(x_hi, f + 1)
                    pe.wait_ge(x_lo, f + 1)
                    for c in range(DC):
                        mm = three_parts(ps[:, 2, :], lambda p: wa[:, p, c * P:(c + 1) * P], lambda p: xs[:, p, c, :],
                                         c == 0, c == DC - 1)
                    mm.then_inc(down_ready, 1)

                def s_up(f, first):
                    pe.wait_ge(down_hi, f + 1)
                    pe.wait_ge(down_lo, f + 1)
                    pe.wait_ge(xr_copied, DC * f + DC)
                    for m in range(DC):
                        three_parts(ps[:, m, :], lambda p: wa[:, p, D + m * P:D + (m + 1) * P], lambda p: dns[:, p, :],
                                    True, True).then_inc(up_ready, 1)

                def s_sum(f, first):
                    pe.wait_ge(x1_sqsum, f + 1)
                    pe.matmul(ps[:, 2, :], ones[:], xn[:, 0, :], start=True, stop=True).then_inc(sum_ready, 1)

                def s_qkv(f, first):
                    pe.wait_ge(xn_hi, f + 1)
                    pe.wait_ge(xn_lo, f + 1)
                    for w in range(2):
                        for m in range(DC):
                            for c in range(DC):
                                mm = three_parts(ps[:, 2 * w + m, :], lambda p: wqk[:, w, p, c, m * P:(m + 1) * P],
                                                 lambda p: xs[:, p, c, :], c == 0, c == DC - 1)
                            mm.then_inc(k_ready if w else q_ready, 1)
                    pe.wait_ge(xn_ready, f + 1)
                    pe.wait_ge(qk_copied, 4 * f + 2)
                    for t in range(NT):
                        for c in range(DC):
                            mm = pe.matmul(ps[:, t // 2, (t % 2) * D:(t % 2 + 1) * D], xn[:, c, t * P:(t + 1) * P], wv[:, c, :],
                                           start=(c == 0), stop=(c == DC - 1))
                        if t % 2:
                            mm.then_inc(v_ready, 1)

                def maxima(b, step):
                    for kind, m in entries(step):
                        e = number[(kind, m)]
                        bank = 2 * (e % 2)
                        if e >= 2:
                            pe.wait_ge(max_read, NENT * b + e - 1)
                        if kind == "turn":
                            pe.wait_ge(max_read, NENT * b + number[("unit", 8 * m + 7)] + 1)
                            pe.transpose(ps[0:16, bank, 0:P], negmax[:, 4 * m:4 * m + 4, :].rearrange("p h t -> p (h t)"),
                                         ident[:]).then_inc(max_ready, 1)
                            continue
                        r0, hh = group_of(m // 2)
                        for i in range(2):
                            t = 2 * (m % 2) + i
                            mm = pe.matmul(ps[:, bank + i, :], qst[r0:r0 + 48, hh, t * P:(t + 1) * P], kst[r0:r0 + 48, hh, :],
                                           start=True, stop=True)
                        mm.then_inc(max_ready, 1)

                def s_max(f, first):
                    pe.wait_ge(stack_loaded, 192 * f + 192)
                    pe.wait_ge(qk_copied, 4 * f + 4)
                    pe.wait_ge(v_copied, 2 * f + 2)
                    maxima(f, -1)

                def scores(b, s):
                    g, kt = divmod(s, 4)
                    if kt == 0:
                        pe.wait_ge(max_loaded[g % 2], 32 * b + 16 * (g // 2) + 16)
                    for j in range(4):
                        t = 4 * s + j
                        if t >= 3:
                            pe.wait_ge(exp_done, 64 * b + t - 2)
                        r0, hh = group_of(4 * g + j)
                        pe.matmul(ps[:, 4 + t % 3, :], kst[r0:r0 + 64, hh, kt * P:(kt + 1) * P], qst[r0:r0 + 64, hh, :],
                                  start=True, stop=True).then_inc(score_ready, 1)

                def values(b, s):
                    g, kt = divmod(s, 4)
                    pe.wait_ge(exp_done, 64 * b + 4 * s + 4)
                    if kt == 0 and g >= 1:
                        pe.wait_ge(u_copied, G * b + g)
                    for j in range(4):
                        mm = pe.matmul(ps[32 * j:32 * j + 32, 7, :], vaug[:, kt, 4 * g + j, :], probs[:, s % NPR, j, :],
                                       start=(kt == 0), stop=(kt == 3), skip_group_check=True)
                    mm.then_inc(pv_done, 1)

                def s_out_proj(b):
                    pe.wait_ge(o_hi, G * b + G)
                    pe.wait_ge(o_lo, G * b + G)
                    for m in range(DC):
                        for g in range(G):
                            mm = three_parts(ps[:, 6 + m, :], lambda p: wo[:, p, g, m * P:(m + 1) * P], lambda p: os_[:, p, g, :],
                                             g == 0, g == G - 1)
                        mm.then_inc(wo_ready, 1)

                def s_back_sum(b):
                    pe.wait_ge(x2_sqsum, b + 1)
                    pe.matmul(ps[:, 4, :], ones[:], yn[:, 0, :], start=True, stop=True).then_inc(x2_sum, 1)

                def out_chunk(b, f):
                    pe.wait_ge(act_hi, FC * b + f + 1)
                    pe.wait_ge(act_lo, FC * b + f + 1)
                    for m in range(DC):
                        mm = three_parts(ps[:, 6 + m, :], lambda p: ow[:, p, f, m * P:(m + 1) * P], lambda p: acts[:, p, f % 2, :],
                                         f == 0, f == FC - 1)
                    mm.then_inc(outc_done, 1)

                def s_ffn(b, f):
                    if f == 0:
                        pe.wait_ge(y_hi, b + 1)
                        pe.wait_ge(y_lo, b + 1)
                    for w, bank, ready, read in ((gw, 4, gate_ready, silu_done), (hw, 5, hid_ready, act_ready)):
                        if f >= 1:
                            pe.wait_ge(read, FC * b + f)
                        for c in range(DC):
                            mm = three_parts(ps[:, bank, :], lambda p: w[:, p, c, f * P:(f + 1) * P], lambda p: ys[:, p, c, :],
                                             c == 0, c == DC - 1)
                        mm.then_inc(ready, 1)
                    if f >= 1:
                        out_chunk(b, f - 1)

                def s_result(b):
                    pe.wait_ge(x3_ready, DC * b + DC)
                    for t in range(NT):
                        for c in range(DC):
                            mm = pe.transpose(ps[:, 6 + t // 2, (t % 2) * D + c * P:(t % 2) * D + (c + 1) * P],
                                              xb[:, c, t * P:(t + 1) * P], ident[:])
                        if t % 2:
                            mm.then_inc(outT_ready, 1)
                    pe.wait_ge(out_copied, 2 * b + 2)

                front = {"xT": s_xT, "down": s_down, "up": s_up, "sum": s_sum, "qkv": s_qkv, "max": s_max}

                def body(b, more):
                    for s in range(STEPS):
                        scores(b, s)
                        maxima(b, s)
                        if s >= 1:
                            values(b, s - 1)
                        for stage in FRONT_IN_ATT.get(s, ()) if more else ():
                            if stage in front:
                                front[stage](b + 1, False)
                    values(b, STEPS - 1)
                    for stage in MID:
                        if stage in front and more:
                            front[stage](b + 1, False)
                        if stage == "out_proj":
                            s_out_proj(b)
                        if stage == "back_sum":
                            s_back_sum(b)
                        if stage[:3] == "ffn" and stage != "ffn_out":
                            s_ffn(b, int(stage[3]))
                        if stage == "ffn_out":
                            out_chunk(b, FC - 1)
                        if stage == "result":
                            s_result(b)

                for stage in FRONT:
                    if stage in front:
                        front[stage](0, True)
                with pe.Fori(0, B - 1) as b:
                    body(b, True)
                body(B - 1, False)

            @block.scalar
            def _(sc):
                def s_sum(f, first):
                    sc.wait_ge(sum_ready, f + 1)
                    nc.scalar.activation(rs[:], ps[:, 2, :], ACT.Sqrt, bias=epsc[:, 0:1], scale=1.0 / D).then_inc(x1_root, 1)

                def s_qkv(f, first):
                    for w, ready in ((0, q_ready), (1, k_ready)):
                        for m in range(DC):
                            sc.wait_ge(ready, DC * f + m + 1)
                            if w == 1:
                                sc.wait_ge(qk_lo, 4 * f + m + 1)
                                sc.wait_ge(qk_hi, 4 * f + m + 1)
                            elif not first:
                                sc.wait_ge(qk_lo, 4 * f)
                                sc.wait_ge(qk_hi, 4 * f)
                            nc.scalar.copy(qkf[:, m, :], ps[:, 2 * w + m, :]).then_inc(qk_copied, 1)

                def exps(b, s, j):
                    t = 4 * s + j
                    sc.wait_ge(score_ready, 64 * b + t + 1)
                    if j == 0 and s >= NPR:
                        sc.wait_ge(pv_done, STEPS * b + s - NPR + 1)
                    nc.scalar.activation(probs[:, s % NPR, j, :], ps[:, 4 + t % 3, :], ACT.Exp, scale=SCALE).then_inc(exp_done, 1)

                def u_copy(b, g):
                    sc.wait_ge(pv_done, STEPS * b + 4 * g + 4)
                    if g >= 1:
                        sc.wait_ge(o_hi, G * b + g)
                        sc.wait_ge(o_lo, G * b + g)
                    nc.scalar.copy(u[:], ps[:, 7, :]).then_inc(u_copied, 1)

                def s_back_sum(b):
                    sc.wait_ge(x2_sum, b + 1)
                    nc.scalar.activation(rsb[:], ps[:, 4, :], ACT.Sqrt, bias=epsc[:, 0:1], scale=1.0 / D).then_inc(x2_root, 1)

                def s_ffn(b, f):
                    sc.wait_ge(gate_ready, FC * b + f + 1)
                    if f >= 1:
                        sc.wait_ge(act_ready, FC * b + f)
                    nc.scalar.activation(sg[:], ps[:, 4, :], ACT.Silu).then_inc(silu_done, 1)

                def s_result(b):
                    for i in range(2):
                        sc.wait_ge(outT_ready, 2 * b + i + 1)
                        nc.scalar.copy(onat[:, 2 * i:2 * i + 2, :].rearrange("p t d -> p (t d)"), ps[:, 6 + i, :]).then_inc(out_copied, 1)

                front = {"sum": s_sum, "qkv": s_qkv}

                def body(b, more, first):
                    sc.wait_ge(x1_ready, DC * b + DC)
                    if not first:
                        sc.wait_ge(outT_ready, 2 * b)
                    nc.scalar.copy(xb[:], xr[:]).then_inc(x1_moved, 1)
                    if not first:
                        sc.wait_ge(out_stored, 16 * b)
                    for s in range(STEPS):
                        for j in range(4):
                            exps(b, s, j)
                            if j == 0 and s % 4 == 1 and s > 4:
                                u_copy(b, s // 4 - 1)
                        for stage in FRONT_IN_ATT.get(s, ()) if more else ():
                            if stage in front:
                                front[stage](b + 1, False)
                    u_copy(b, G - 1)
                    for stage in MID:
                        if stage in front and more:
                            front[stage](b + 1, False)
                        if stage == "back_sum":
                            s_back_sum(b)
                        if stage[:3] == "ffn" and stage != "ffn_out":
                            s_ffn(b, int(stage[3]))
                        if stage == "result":
                            s_result(b)

                for stage in FRONT:
                    if stage in front:
                        front[stage](0, True)
                body(0, True, True)
                with sc.Fori(1, B - 1) as b:
                    body(b, True, False)
                body(B - 1, False, False)

            @block.vector
            def _(dve):
                def s_xT(f, first):
                    if not first:
                        dve.wait_ge(x1_moved, f)
                    for c in range(DC):
                        dve.wait_ge(xT_ready, DC * f + c + 1)
                        nc.vector.tensor_copy(xr[:, c, :], ps[:, c, :]).then_inc(xr_copied, 1)
                    dve.wait_ge(xr_copied, DC * f + DC)
                    if not first:
                        dve.wait_ge(k_ready, DC * f)
                    nc.vector.tensor_copy(xs[:, 0], xr[:]).then_inc(x_hi, 1)

                def s_down(f, first):
                    dve.wait_ge(down_ready, f + 1)
                    nc.vector.tensor_scalar(dn[:], ps[:, 2, :], bdc[:, 0:1], 0.0, ALU.add, ALU.max).then_inc(down_act, 1)
                    dve.wait_ge(down_act, f + 1)
                    nc.vector.tensor_copy(dns[:, 0], dn[:]).then_inc(down_hi, 1)

                def s_up(f, first):
                    for m in range(DC):
                        dve.wait_ge(up_ready, DC * f + m + 1)
                        dve.wait_ge(x_lo, f + 1)
                        nc.vector.scalar_tensor_tensor(xr[:, m, :], ps[:, m, :], buc[:, m:m + 1], xr[:, m, :],
                                                       ALU.add, ALU.add).then_inc(x1_ready, 1)
                    dve.wait_ge(x1_ready, DC * f + DC)
                    if not first:
                        dve.wait_ge(v_ready, 2 * f)
                    nc.vector.tensor_tensor(xn[:], xr[:], xr[:], ALU.mult).then_inc(x1_sq, 1)
                    dve.wait_ge(x1_sq, f + 1)
                    nc.vector.tensor_tensor(xn[:, 0, :], xn[:, 0, :], xn[:, 1, :], ALU.add).then_inc(x1_sqsum, 1)

                def s_norm(f, first):
                    dve.wait_ge(x1_root, f + 1)
                    nc.vector.reciprocal(rs[:], rs[:]).then_inc(x1_rs, 1)
                    dve.wait_ge(x1_rs, f + 1)
                    for c in range(DC):
                        nc.vector.tensor_tensor(xn[:, c, :], xr[:, c, :], rs[:], ALU.mult).then_inc(xn_scaled, 1)
                    for c in range(DC):
                        dve.wait_ge(xn_scaled, DC * f + c + 1)
                        nc.vector.tensor_scalar(xn[:, c, :], xn[:, c, :], cvec(A_GAMMA, f, c), cvec(A_BETA, f, c),
                                                ALU.mult, ALU.add).then_inc(xn_ready, 1)
                    dve.wait_ge(xn_ready, DC * f + DC)
                    nc.vector.tensor_copy(xs[:, 0], xn[:]).then_inc(xn_hi, 1)

                def s_qkv(f, first):
                    for w in range(2):
                        for m in range(DC):
                            dve.wait_ge(qk_copied, 4 * f + 2 * w + m + 1)
                            if m == 0 and w == 1:
                                dve.wait_ge(parts_stored[0], 16 * f + 16)
                            if m == 0 and w == 0 and not first:
                                dve.wait_ge(parts_stored[1], 16 * f)
                            nc.vector.tensor_copy(qks[:, 0, m, :], qkf[:, m, :]).then_inc(qk_hi, 1)
                    if not first:
                        dve.wait_ge(pv_done, STEPS * f)
                    for i in range(2):
                        dve.wait_ge(v_ready, 2 * f + i + 1)
                        nc.vector.tensor_copy(vaug[:, 2 * i:2 * i + 2, :, 0:DH],
                                              ps[:, i, :].rearrange("p (t h d) -> p t h d", t=2, h=NH)).then_inc(v_copied, 1)

                def maxima(b, step):
                    for kind, m in entries(step):
                        e = number[(kind, m)]
                        bank = 2 * (e % 2)
                        dve.wait_ge(max_ready, NENT * b + e + 1)
                        if kind == "turn":
                            nc.vector.tensor_copy(negrow[:, m, :], ps[0:16, bank, 0:P]).then_inc(max_read, 1)
                        else:
                            h, t = m // 2, 2 * (m % 2)
                            nc.vector.tensor_reduce(negmax[:, h, t:t + 2], ps[:, bank:bank + 2, :], AX_X, ALU.max,
                                                    negate=True).then_inc(max_read, 1)

                def s_max(f, first):
                    maxima(f, -1)

                def o_scale(b, g):
                    dve.wait_ge(u_copied, G * b + g + 1)
                    if g >= 1:
                        dve.wait_ge(o_scaled, G * b + g)
                    dve.sem_inc(passed_v, 1)
                    nc.vector.stream_shuffle(den[:], u[:], [16 + i % 16 for i in range(32)]).then_inc(den_ready, 1)
                    dve.wait_ge(den_ready, G * b + g + 1)
                    nc.vector.reciprocal(den[:], den[:]).then_inc(rden_ready, 1)

                def s_out_proj(b):
                    for m in range(DC):
                        dve.wait_ge(wo_ready, DC * b + m + 1)
                        dve.wait_ge(x1_moved, b + 1)
                        nc.vector.scalar_tensor_tensor(xb[:, m, :], ps[:, 6 + m, :], cvec(A_ALPHA, b, m), xb[:, m, :],
                                                       ALU.mult, ALU.add).then_inc(x2_ready, 1)
                    dve.wait_ge(x2_ready, DC * b + DC)
                    nc.vector.tensor_tensor(yn[:], xb[:], xb[:], ALU.mult).then_inc(x2_sq, 1)
                    dve.wait_ge(x2_sq, b + 1)
                    nc.vector.tensor_tensor(yn[:, 0, :], yn[:, 0, :], yn[:, 1, :], ALU.add).then_inc(x2_sqsum, 1)

                def s_back_norm(b):
                    dve.wait_ge(x2_root, b + 1)
                    nc.vector.reciprocal(rsb[:], rsb[:]).then_inc(x2_rs, 1)
                    dve.wait_ge(x2_rs, b + 1)
                    for c in range(DC):
                        nc.vector.tensor_tensor(yn[:, c, :], xb[:, c, :], rsb[:], ALU.mult).then_inc(yn_scaled, 1)
                    for c in range(DC):
                        dve.wait_ge(yn_scaled, DC * b + c + 1)
                        nc.vector.tensor_scalar(yn[:, c, :], yn[:, c, :], cvec(F_GAMMA, b, c), cvec(F_BETA, b, c),
                                                ALU.mult, ALU.add).then_inc(yn_ready, 1)
                    dve.wait_ge(yn_ready, DC * b + DC)
                    nc.vector.tensor_copy(ys[:, 0], yn[:]).then_inc(y_hi, 1)

                def s_ffn(b, f):
                    dve.wait_ge(hid_ready, FC * b + f + 1)
                    dve.wait_ge(silu_done, FC * b + f + 1)
                    if f >= 2:
                        dve.wait_ge(outc_done, FC * b + f - 1)
                        dve.wait_ge(act_lo, FC * b + f - 1)
                    nc.vector.tensor_tensor(act[:, f % 2, :], ps[:, 5, :], sg[:], ALU.mult).then_inc(act_ready, 1)
                    dve.wait_ge(act_ready, FC * b + f + 1)
                    nc.vector.tensor_copy(acts[:, 0, f % 2, :], act[:, f % 2, :]).then_inc(act_hi, 1)

                def s_ffn_out(b):
                    dve.wait_ge(outc_done, FC * b + FC)
                    for m in range(DC):
                        if m == 1:
                            dve.wait_ge(x3_ready, DC * b + 1)
                        nc.vector.tensor_scalar(tmp[:], ps[:, 6 + m, :], obc[:, m:m + 1], cvec(F_ALPHA, b, m),
                                                ALU.add, ALU.mult).then_inc(ffn_scaled, 1)
                        dve.wait_ge(ffn_scaled, DC * b + m + 1)
                        nc.vector.tensor_tensor(xb[:, m, :], xb[:, m, :], tmp[:], ALU.add).then_inc(x3_ready, 1)

                front = {"xT": s_xT, "down": s_down, "up": s_up, "norm": s_norm, "qkv": s_qkv, "max": s_max}

                def body(b, more):
                    for s in range(STEPS):
                        maxima(b, s)
                        if s % 4 == 1 and s > 4:
                            o_scale(b, s // 4 - 1)
                        for stage in FRONT_IN_ATT.get(s, ()) if more else ():
                            if stage in front:
                                front[stage](b + 1, False)
                    o_scale(b, G - 1)
                    for stage in MID:
                        if stage in front and more:
                            front[stage](b + 1, False)
                        if stage == "out_proj":
                            s_out_proj(b)
                        if stage == "back_norm":
                            s_back_norm(b)
                        if stage[:3] == "ffn" and stage != "ffn_out":
                            s_ffn(b, int(stage[3]))
                        if stage == "ffn_out":
                            s_ffn_out(b)

                for c in range(DC):
                    for st in (kst, qst):
                        nc.vector.memset(st[64 * c + 32:64 * c + 64].bitcast(F32), 0.0).then_inc(stack_zeroed, 1)
                nc.vector.memset(vaug[:, :, :, DH:32], 1.0).then_inc(vones, 1)
                for stage in FRONT:
                    if stage in front:
                        front[stage](0, True)
                with dve.Fori(0, B - 1) as b:
                    body(b, True)
                body(B - 1, False)

            @block.gpsimd
            def _(pool):
                def s_xT(f, first):
                    pool.wait_ge(dw_loaded, 64 * f + 64)
                    if not first:
                        pool.wait_ge(up_ready, DC * f)
                    nc.gpsimd.tensor_tensor(wa[:, 0], dwl[:], base[:], ALU.add).then_inc(adapter_w, 1)
                    pool.wait_ge(adapter_w, 3 * f + 1)
                    nc.gpsimd.tensor_tensor(dwl[:], dwl[:], base[:], ALU.add).then_inc(adapter_w, 1)
                    pool.wait_ge(adapter_w, 3 * f + 2)
                    nc.gpsimd.tensor_tensor(wa[:, 1], dwl[:], wa[:, 0], ALU.subtract).then_inc(adapter_w, 1)
                    pool.wait_ge(x_hi, f + 1)
                    nc.gpsimd.tensor_tensor(xs[:, 1], xr[:], xs[:, 0], ALU.subtract).then_inc(x_lo, 1)

                def s_down(f, first):
                    pool.wait_ge(down_hi, f + 1)
                    nc.gpsimd.tensor_tensor(dns[:, 1], dn[:], dns[:, 0], ALU.subtract).then_inc(down_lo, 1)

                def s_norm(f, first):
                    pool.wait_ge(xn_hi, f + 1)
                    nc.gpsimd.tensor_tensor(xs[:, 1], xn[:], xs[:, 0], ALU.subtract).then_inc(xn_lo, 1)

                def s_qkv(f, first):
                    for w in range(2):
                        for m in range(DC):
                            pool.wait_ge(qk_hi, 4 * f + 2 * w + m + 1)
                            nc.gpsimd.tensor_tensor(qks[:, 1, m, :], qkf[:, m, :], qks[:, 0, m, :], ALU.subtract).then_inc(qk_lo, 1)

                def o_split(b, g):
                    pool.wait_ge(rden_ready, G * b + g + 1)
                    nc.gpsimd.tensor_tensor(os_[:, 0, g, :], u[:], den[:], ALU.mult).then_inc(o_hi, 1)
                    pool.wait_ge(o_hi, G * b + g + 1)
                    nc.gpsimd.tensor_tensor(u[:], u[:], den[:], ALU.mult).then_inc(o_scaled, 1)
                    pool.wait_ge(o_scaled, G * b + g + 1)
                    nc.gpsimd.tensor_tensor(os_[:, 1, g, :], u[:], os_[:, 0, g, :], ALU.subtract).then_inc(o_lo, 1)

                def s_back_norm(b):
                    pool.wait_ge(y_hi, b + 1)
                    nc.gpsimd.tensor_tensor(ys[:, 1], yn[:], ys[:, 0], ALU.subtract).then_inc(y_lo, 1)

                def s_ffn(b, f):
                    pool.wait_ge(act_hi, FC * b + f + 1)
                    nc.gpsimd.tensor_tensor(acts[:, 1, f % 2, :], act[:, f % 2, :], acts[:, 0, f % 2, :],
                                            ALU.subtract).then_inc(act_lo, 1)

                front = {"xT": s_xT, "down": s_down, "norm": s_norm, "qkv": s_qkv}

                def body(b, more, first):
                    for s in range(STEPS):
                        if s % 4 == 1 and s > 4:
                            o_split(b, s // 4 - 1)
                        for stage in FRONT_IN_ATT.get(s, ()) if more else ():
                            if stage in front:
                                front[stage](b + 1, False)
                    o_split(b, G - 1)
                    for stage in MID:
                        if stage in front and more:
                            front[stage](b + 1, False)
                        if stage == "back_norm":
                            s_back_norm(b)
                        if stage[:3] == "ffn" and stage != "ffn_out":
                            s_ffn(b, int(stage[3]))

                for stage in FRONT:
                    if stage in front:
                        front[stage](0, True)
                body(0, True, True)
                with pool.Fori(1, B - 1) as b:
                    body(b, True, False)
                body(B - 1, False, False)


_CONDS = ["L1_cond_attn_gamma_w", "L1_cond_attn_beta_w", "L1_cond_attn_alpha_w",
          "L1_cond_ffn_gamma_w", "L1_cond_ffn_beta_w", "L1_cond_ffn_alpha_w"]
_FIRST = ["x", "cond_256", "L0_cond_Wd", "L0_cond_bd", "L0_cond_Wu", "L0_cond_bu", "L0_cond_Wdd", "L0_cond_bdd",
          "L0_cond_Wdu", "L0_cond_bdu"]
_LAST = ["L1_cond_W_q", "L1_cond_W_k", "L1_cond_W_v", "L1_cond_W_o", "L1_cond_gate_w", "L1_cond_hidden_w",
         "L1_cond_out_w", "L1_cond_out_b"]


def kernel(**inputs):
    import concourse.bacc as bacc
    from concourse.bass_utils import run_bass_kernel_spmd

    nc = bacc.Bacc("TRN2", target_bir_lowering=False, num_devices=1)
    arrays = {}

    def given(name):
        a = np.ascontiguousarray(inputs[name])
        arrays[f"in_{name}"] = a
        return nc.dram_tensor(f"in_{name}", a.shape, mybir.dt.from_np(a.dtype), kind="ExternalInput").ap()

    first = [given(n) for n in _FIRST]
    conds = [given(n) for n in _CONDS]
    last = [given(n) for n in _LAST]
    out = nc.dram_tensor("out", inputs["x"].shape, F32, kind="ExternalOutput").ap()
    adapter_block_kernel(nc, *first, conds, *last, out)
    r = run_bass_kernel_spmd(nc, [arrays], core_ids=[0])
    return r.results[0]["out"]
```

```python
import numpy as np
import concourse.bass as bass
from concourse import mybir
from contextlib import ExitStack

F32, F32R, BF16 = mybir.dt.float32, mybir.dt.float32r, mybir.dt.bfloat16
ALU = mybir.AluOpType
ACT = mybir.ActivationFunctionType
AX_X = mybir.AxisListType.X

P = 128
EPS = 1e-6
DELTA = 0.1
GATED_HI_LO = ((0, 0), (1, 0), (0, 1))


def adapter_block_kernel(nc, x, cond, Wd, bd, Wu, bu, Wdd, bdd, Wdu, bdu, cond_ws, Wq, Wk, Wv, Wo,
                         gate_w, hidden_w, out_w, out_b, out):
    B, L, D = x.shape
    BN = Wd.shape[0]
    HC = cond.shape[1]
    DH = 16
    NH = D // DH
    F = gate_w.shape[0]
    DC = D // P
    FC = F // P
    NT = L // P
    G = NH // 4
    HH = NH // DC
    SCALE = (NH / D) ** 0.5
    assert BN == P and HC == 64 and L == 512 and DC == 2 and NT == 4 and G == 4

    with ExitStack() as ctx:
        def sem(name):
            return ctx.enter_context(nc.semaphore(name))

        end_of = [16512]

        def place(name, shape, dt=F32, at=None):
            size = (2 if dt == BF16 else 4) * int(np.prod(shape[1:]))
            start = end_of[0] if at is None else at
            if at is None:
                end_of[0] = -(-(start + size) // 32) * 32
            assert start + size <= 229344, (name, start + size)
            return nc.alloc_sbuf_tensor_at(name, shape, dt, offset=start)

        ps = ctx.enter_context(nc.psum_tensor("ps", [P, 8, 512], F32))
        dw_scr = nc.dram_tensor("dw_scr", (2, 8, 2, 64, P), F32).ap()
        qk_scr = nc.dram_tensor("qk_scr", (2, 3, D, L), BF16).ap()

        ident = place("ident", [P, P])
        ones = place("ones", [P, 1])
        ones_bf = place("ones_bf", [P, P], BF16)
        bdc = place("bdc", [P, 1])
        buc = place("buc", [P, DC])
        obc = place("obc", [P, DC])
        conds = place("conds", [P, 6, 8])
        base = place("base", [P, 512])
        wqk = place("wqk", [P, 2, 2, DC, D], F32R)
        wv = place("wv", [P, DC, D])
        wo = place("wo", [P, 2, G, D], F32R)
        gw = place("gw", [P, 2, DC, F], F32R)
        hw = place("hw", [P, 2, DC, F], F32R)
        ow = place("ow", [P, 2, FC, D], F32R)
        loop_base = end_of[0]

        NST = 4
        dd_in = place("dd_in", [P, NST, 2048])
        ddT = place("ddT", [P, 2, 4, 512])
        dw_out = place("dw_out", [P, 2, 4, 512])
        qkvo_in = place("qkvo_in", [P, 4, DC, D])
        wo_pad = place("wo_pad", [P, DC, G, 4, 32])
        gh_in = place("gh_in", [P, 2, FC, D])
        ow_in = place("ow_in", [P, DC, F])
        base_in = place("base_in", [P, 512])
        bias_in = place("bias_in", [P, 512])
        cw_in = place("cw_in", [P, 6, 2, HC])
        cwT = place("cwT", [P, 6, P])
        csel = place("csel", [P, 32])
        assert end_of[0] <= 229344

        end_of[0] = loop_base
        Q_PARTS, K_PARTS = (0, 0, 1, 1, 0, 2), (0, 1, 0, 1, 2, 0)
        KMAX, KALL = 6 * DH, 6 * DH + 2
        kst = place("kst", [P, NH, L], BF16)
        qst = place("qst", [P, NH, L], BF16)
        NPR = 3
        probs_at = end_of[0]
        probs = place("probs", [P, NPR, 4, L])
        vaug = place("vaug", [P, NT, NH, 32])
        xnat = place("xnat", [P, NT, D])
        xr = place("xr", [P, DC, L])
        xs = place("xs", [P, 2, DC, L], F32R)
        dn = place("dn", [P, L])
        dns = place("dns", [P, 2, L], F32R)
        xn = place("xn", [P, DC, L])
        dwl = place("dwl", [P, 512])
        wa = place("wa", [P, 2, 512], F32R)
        qkf = place("qkf", [P, DC, L])
        qks = place("qks", [P, 3, DC, L], BF16)
        negmax = place("negmax", [P, NH, NT])
        negrow = place("negrow", [16, G, 2, P], BF16)
        negrest = place("negrest", [16, P])
        rst = place("rst", [P, 2, 3, NT])
        nwt = place("nwt", [P, 2, NT])
        rden = place("rden", [P, NT, 4])
        rden_rows = place("rden_rows", [P, NT, 4, 32])
        u = place("u", [P, L])
        xb = place("xb", [P, DC, L])
        os_at = end_of[0]
        os_ = place("os_", [P, 2, G, L], F32R)
        act = place("act", [P, 2, L], at=os_at)
        acts = place("acts", [P, 2, 2, L], F32R, at=os_at + 4096)
        onat = place("onat", [P, NT, D], at=os_at + 12288)
        ys = place("ys", [P, 2, DC, L], F32R, at=probs_at)
        yn = place("yn", [P, DC, L], at=probs_at + 8192)
        sg = place("sg", [P, L], at=probs_at + 12288)
        tmp = place("tmp", [P, L], at=probs_at + 14336)

        groups = ["cond0", "cond1", "condm", "base", "q", "k", "v", "o0", "o1"]
        groups += [f"{w}{k}{half}" for w in "gh" for k in range(DC) for half in range(2)]
        groups += [f"w{p}" for p in range(FC // 2)]
        loads_of = {"cond0": "cw", "cond1": "cw", "condm": "cond", "base": "base"}
        NCH = 16
        first_group = [-(-c * len(groups) // NCH) for c in range(NCH + 1)]

        dd_loaded = sem("dd_loaded")
        dd_loaded = [dd_loaded] + [sem(f"dd_loaded{i}") for i in range(1, NST)]
        w_loaded = {n: sem(f"w_loaded_{n}") for n in ("cond", "cw", "base", "qkvo", "gate", "hidden", "outw", "vec")}
        const_ready = sem("const_ready")
        base_summed = sem("base_summed")
        pad_ready = sem("pad_ready")
        ddT_ready = sem("ddT_ready")
        ddT_copied_a = sem("ddT_copied_a")
        ddT_copied_v = sem("ddT_copied_v")
        dw_ready = sem("dw_ready")
        dw_copied = sem("dw_copied")
        dw_stored = [sem("dw_stored0"), sem("dw_stored1")]
        wt_ready = sem("wt_ready")
        wt_hi = sem("wt_hi")
        wt_copied = sem("wt_copied")
        cwT_copied = sem("cwT_copied")

        def blocks_of(g):
            if g == "cond0":
                return [(cw_in[:, k, :, :].rearrange("p e h -> p (e h)"), k * P) for k in range(4)]
            if g == "cond1":
                return [(cw_in[:, k, :, :].rearrange("p e h -> p (e h)"), (k - 4) * P) for k in range(4, 6)]
            if g == "base":
                return [(base_in[:, i * P:(i + 1) * P], i * P) for i in range(4)]
            if g in "qkv":
                i = "qkv".index(g)
                return [(qkvo_in[:, i, m, k * P:(k + 1) * P], k * D + m * P) for k in range(DC) for m in range(DC)]
            if g[0] == "o":
                return [(wo_pad[:, m, 2 * int(g[1]) + i, :, :].rearrange("p j r -> p (j r)"), i * D + m * P)
                        for i in range(2) for m in range(DC)]
            if g[0] in "gh":
                w, k, half = "gh".index(g[0]), int(g[1]), int(g[2])
                return [(gh_in[:, w, 4 * half + i, k * P:(k + 1) * P], i * P) for i in range(4)]
            p = int(g[1])
            return [(ow_in[:, m, (2 * p + i) * P:(2 * p + i + 1) * P], i * D + m * P)
                    for i in range(2) for m in range(DC)]

        def kept_at(g, part):
            if g in "qk":
                return wqk[:, "qk".index(g), part, :, :].rearrange("p k n -> p (k n)")
            if g[0] == "o":
                i = 2 * int(g[1])
                return wo[:, part, i:i + 2, :].rearrange("p g n -> p (g n)")
            if g[0] in "gh":
                k, half = int(g[1]), int(g[2])
                return (gw if g[0] == "g" else hw)[:, part, k, half * 512:(half + 1) * 512]
            p = int(g[1])
            return ow[:, part, 2 * p:2 * p + 2, :].rearrange("p f n -> p (f n)")

        def load_name(g):
            if g in loads_of:
                return loads_of[g]
            return {"q": "qkvo", "k": "qkvo", "v": "qkvo", "o": "qkvo", "g": "gate", "h": "hidden", "w": "outw"}[g[0]]

        with nc.Block() as block:
            @block.sync
            def _(sp):
                for e in range(2):
                    for b in range(B):
                        if e == 0 and b == 0:
                            sp.wait_ge(const_ready, 1)
                        col = cond[b:b + 1, :].rearrange("b h -> h b")
                        sp.dma_start(csel[e * HC:(e + 1) * HC, 2 * b + e:2 * b + e + 1], col).then_inc(w_loaded["cond"], 16)
                for k, w in enumerate(cond_ws):
                    sp.dma_start(cw_in[:, k], w.rearrange("(e p) h -> p e h", p=P)).then_inc(w_loaded["cw"], 16)

                def chunk(c):
                    if c >= NST:
                        sp.wait_ge(ddT_ready, 4 * (c - NST + 1))
                    if c < NCH // 2:
                        src = Wdd.rearrange("(n d) h -> n (d h)", d=D)[:, c * 2048:(c + 1) * 2048]
                    else:
                        dc, nb = divmod(c - NCH // 2, 4)
                        src = Wdu.rearrange("(dc dp n) h -> dc dp (n h)", dc=DC, n=BN)[dc][:, nb * 2048:(nb + 1) * 2048]
                    sp.dma_start(dd_in[:, c % NST], src).then_inc(dd_loaded[c % NST], 16)

                chunk(0)
                sp.dma_start(base_in[:, 0:D], Wd).then_inc(w_loaded["base"], 16)
                sp.dma_start(base_in[:, D:512], Wu.rearrange("(c p) n -> p c n", p=P)).then_inc(w_loaded["base"], 16)
                sp.dma_start(bias_in[:, 0:D], bdd.rearrange("(n d) -> n d", d=D)).then_inc(w_loaded["base"], 16)
                sp.dma_start(bias_in[:, D:512], bdu.rearrange("(c p n) -> p c n", p=P, n=BN)).then_inc(w_loaded["base"], 16)
                chunk(1)
                for i, w in enumerate((Wq, Wk, Wv, Wo)):
                    sp.dma_start(qkvo_in[:, i], w.rearrange("(m p) k -> p m k", p=P)).then_inc(w_loaded["qkvo"], 16)
                chunk(2)
                sp.dma_start(gh_in[:, 0], gate_w.rearrange("(f p) k -> p f k", p=P)).then_inc(w_loaded["gate"], 16)
                chunk(3)
                sp.dma_start(gh_in[:, 1], hidden_w.rearrange("(f p) k -> p f k", p=P)).then_inc(w_loaded["hidden"], 16)
                sp.dma_start(ow_in[:], out_w.rearrange("(m p) f -> p m f", p=P)).then_inc(w_loaded["outw"], 16)
                sp.dma_start(bdc[:], bd.rearrange("(p o) -> p o", o=1)).then_inc(w_loaded["vec"], 16)
                for c in range(DC):
                    for to, vec in ((buc, bu), (obc, out_b)):
                        src = vec[c * P:(c + 1) * P].rearrange("(p o) -> p o", o=1)
                        sp.dma_start(to[:, c:c + 1], src).then_inc(w_loaded["vec"], 16)
                for c in range(4, NCH):
                    chunk(c)
                sp.wait_ge(w_loaded["vec"], 80)

            @block.gpsimd
            def _(pool):
                nc.gpsimd.memset(csel[:], 0.0).then_inc(const_ready, 1)
                nc.gpsimd.memset(ident[:], 0.0).then_inc(const_ready, 1)
                nc.gpsimd.memset(ones[:], 1.0).then_inc(const_ready, 1)
                nc.gpsimd.memset(ones_bf[:], 1.0).then_inc(const_ready, 1)
                pool.wait_ge(const_ready, 4)
                nc.gpsimd.affine_select(out=ident[:], in_=ident[:], compare_op=ALU.not_equal, fill=1.0, base=0,
                                        pattern=[[-1, P]], channel_multiplier=1).then_inc(const_ready, 1)
                nc.gpsimd.memset(wo_pad[:], 0.0).then_inc(pad_ready, 1)
                pool.wait_ge(w_loaded["base"], 64)
                nc.gpsimd.tensor_scalar(bias_in[:], bias_in[:], DELTA, None, ALU.mult).then_inc(base_summed, 1)
                pool.wait_ge(base_summed, 1)
                nc.gpsimd.tensor_tensor(base_in[:], base_in[:], bias_in[:], ALU.add).then_inc(base_summed, 1)
                pool.wait_ge(w_loaded["qkvo"], 64)
                pool.wait_ge(pad_ready, 1)
                for m in range(DC):
                    nc.gpsimd.tensor_copy(wo_pad[:, m, :, :, 0:DH],
                                          qkvo_in[:, 3, m, :].rearrange("p (g j r) -> p g j r", g=G, j=4)).then_inc(pad_ready, 1)
                for r in range(4):
                    pool.wait_ge(dw_copied, 4 * (r + 1))
                    for g in range(4):
                        dst = dw_scr[r // 2, :, r % 2].rearrange("p (c g j) n -> g p c (j n)", c=4, g=4)[g]
                        pool.dma_start(dst, dw_out[32 * g:32 * g + 8, r % 2]).then_inc(dw_stored[r % 2], 16)
                for s in dw_stored:
                    pool.wait_ge(s, 128)

            @block.tensor
            def _(pe):
                def dd_transposes(c):
                    pe.wait_ge(dd_loaded[c % NST], 16 * (c // NST + 1))
                    for t in range(4):
                        if c >= 1:
                            pe.wait_ge(ddT_copied_v if t < 2 else ddT_copied_a, 2 * (c - 1) + t % 2 + 1)
                        for i in range(4):
                            j = 4 * t + i
                            mm = pe.transpose(ps[:, t, i * P:(i + 1) * P], dd_in[:, c % NST, j * P:(j + 1) * P], ident[:])
                        mm.then_inc(ddT_ready, 1)

                def dd_products(c):
                    pe.wait_ge(ddT_copied_v, 2 * (c + 1))
                    pe.wait_ge(ddT_copied_a, 2 * (c + 1))
                    if c >= 2:
                        pe.wait_ge(dw_copied, c - 1)
                    for t in range(4):
                        mm = pe.matmul(ps[32 * t:32 * t + 32, 4 + c % 2, :], csel[:], ddT[:, c % 2, t, :], start=True, stop=True)
                    mm.then_inc(dw_ready, 1)

                def weights(i):
                    g = groups[i]
                    if g == "condm":
                        pe.wait_ge(cwT_copied, 2)
                        pe.wait_ge(w_loaded["cond"], 128)
                        if i >= 2:
                            pe.wait_ge(wt_copied, i - 1)
                        for k in range(6):
                            mm = pe.matmul(ps[:, 6 + i % 2, 32 * k:32 * k + 32], cwT[:, k, :], csel[:], start=True, stop=True)
                        mm.then_inc(wt_ready, 1)
                        return
                    if g == "base":
                        pe.wait_ge(base_summed, 2)
                    elif g[0] == "o":
                        pe.wait_ge(pad_ready, 1 + DC)
                    else:
                        pe.wait_ge(w_loaded[load_name(g)], {"cw": 96, "qkvo": 64}.get(load_name(g), 16))
                    if i >= 2:
                        pe.wait_ge(wt_copied, i - 1)
                    for src, col in blocks_of(g):
                        mm = pe.transpose(ps[:, 6 + i % 2, col:col + P], src, ident[:])
                    mm.then_inc(wt_ready, 1)

                pe.wait_ge(const_ready, 5)
                for c in range(NCH):
                    if c == 1:
                        pe.wait_ge(w_loaded["cond"], 128)
                    dd_transposes(c)
                    for i in range(first_group[c], first_group[c + 1]):
                        weights(i)
                    if c >= 1:
                        dd_products(c - 1)
                dd_products(NCH - 1)

            @block.scalar
            def _(act_):
                for c in range(NCH + 1):
                    if c < NCH:
                        if c >= 2:
                            act_.wait_ge(dw_ready, c - 1)
                        for t in (2, 3):
                            act_.wait_ge(ddT_ready, 4 * c + t + 1)
                            nc.scalar.copy(ddT[:, c % 2, t, :], ps[:, t, :]).then_inc(ddT_copied_a, 1)
                    if c >= 1:
                        act_.wait_ge(dw_ready, c)
                        if c > 8:
                            act_.wait_ge(dw_stored[(c - 1) // 4 % 2], 64)
                        nc.scalar.mul(dw_out[:, (c - 1) // 4 % 2, (c - 1) % 4, :], ps[:, 4 + (c - 1) % 2, :], DELTA).then_inc(dw_copied, 1)

            @block.vector
            def _(dve):
                def copy_weights(i):
                    g, bank = groups[i], 6 + i % 2
                    dve.wait_ge(wt_ready, i + 1)
                    if g == "cond0":
                        nc.vector.tensor_copy(cwT[:, 0:4, :].rearrange("p k n -> p (k n)"), ps[:, bank, :]).then_inc(cwT_copied, 1)
                        dve.wait_ge(cwT_copied, 1)
                        nc.vector.engine_nop().then_inc(wt_copied, 1)
                    elif g == "cond1":
                        nc.vector.tensor_copy(cwT[:, 4:6, :].rearrange("p k n -> p (k n)"), ps[:, bank, 0:2 * P]).then_inc(cwT_copied, 1)
                        dve.wait_ge(cwT_copied, 2)
                        nc.vector.engine_nop().then_inc(wt_copied, 1)
                    elif g == "condm":
                        src = ps[:, bank, 0:192].rearrange("p (k n) -> p k n", k=6)[:, :, 0:8]
                        nc.vector.tensor_copy(conds[:], src).then_inc(wt_copied, 1)
                    elif g == "base":
                        nc.vector.tensor_copy(base[:], ps[:, bank, :]).then_inc(wt_copied, 1)
                    elif g == "v":
                        nc.vector.tensor_copy(wv[:].rearrange("p k n -> p (k n)"), ps[:, bank, :]).then_inc(wt_copied, 1)
                    else:
                        nc.vector.tensor_copy(kept_at(g, 0), ps[:, bank, :]).then_inc(wt_hi, 1)
                        split[0] += 1
                        dve.wait_ge(wt_hi, split[0])
                        nc.vector.tensor_tensor(kept_at(g, 1), ps[:, bank, :], kept_at(g, 0), ALU.subtract).then_inc(wt_copied, 1)

                split = [0]
                for c in range(NCH):
                    if c >= 2:
                        dve.wait_ge(dw_ready, c - 1)
                    for t in (0, 1):
                        dve.wait_ge(ddT_ready, 4 * c + t + 1)
                        nc.vector.tensor_copy(ddT[:, c % 2, t, :], ps[:, t, :]).then_inc(ddT_copied_v, 1)
                    for i in range(first_group[c], first_group[c + 1]):
                        copy_weights(i)

        x_loaded, dw_loaded = sem("x_loaded"), sem("dw_loaded")
        parts_stored = [sem("q_stored"), sem("k_stored")]
        stack_loaded = sem("stack_loaded")
        max_loaded = [sem("max_loaded0"), sem("max_loaded1")]
        out_stored, stack_ones, vones, passed_s = sem("out_stored"), sem("stack_ones"), sem("vones"), sem("passed_s")
        xT_ready, down_ready, up_ready, sum_ready = sem("xT_ready"), sem("down_ready"), sem("up_ready"), sem("sum_ready")
        x1_rows = sem("x1_rows")
        qk_ready, v_ready = [sem("q_ready"), sem("k_ready")], sem("v_ready")
        xr_copied, x_hi, x_lo, adapter_w = sem("xr_copied"), sem("x_hi"), sem("x_lo"), sem("adapter_w")
        down_act, down_hi, down_lo = sem("down_act"), sem("down_hi"), sem("down_lo")
        x1_moved, x1_ready, x1_sq, x1_sqsum = sem("x1_moved"), sem("x1_ready"), sem("x1_sq"), sem("x1_sqsum")
        xn_scaled, xn_ready, xn_hi, xn_lo = sem("xn_scaled"), sem("xn_ready"), sem("xn_hi"), sem("xn_lo")
        qk_copied, qk_b0, qk_r1, qk_b1, qk_b2, v_copied = (sem("qk_copied"), sem("qk_b0"), sem("qk_r1"), sem("qk_b1"),
                                                           sem("qk_b2"), sem("v_copied"))
        mean_ready = [sem("x1_mean"), sem("x2_mean")]
        root_ready = [sem("x1_root"), sem("x2_root")]
        rroot_step = [sem("x1_rroot"), sem("x2_rroot")]
        max_ready, max_read, neg_hi, neg_rest, neg_lo = (sem("max_ready"), sem("max_read"), sem("neg_hi"), sem("neg_rest"),
                                                         sem("neg_lo"))
        score_ready, exp_done, pv_done = sem("score_ready"), sem("exp_done"), sem("pv_done")
        rden_spread = sem("rden_spread")
        u_copied, den_ready, rden_ready, rec_ready, o_scaled, o_hi, o_lo = (
            sem("u_copied"), sem("den_ready"), sem("rden_ready"), sem("rec_ready"), sem("o_scaled"), sem("o_hi"), sem("o_lo"))
        wo_ready, x2_ready, x2_sq, x2_sqsum, x2_sum = sem("wo_ready"), sem("x2_ready"), sem("x2_sq"), sem("x2_sqsum"), sem("x2_sum")
        x2_rows, yn_scaled, yn_ready, y_hi, y_lo = sem("x2_rows"), sem("yn_scaled"), sem("yn_ready"), sem("y_hi"), sem("y_lo")
        gate_ready, hid_ready, silu_done, act_ready, act_hi, act_lo = (sem("gate_ready"), sem("hid_ready"), sem("silu_done"),
                                                                       sem("act_ready"), sem("act_hi"), sem("act_lo"))
        outc_done, ffn_scaled, x3_ready, outT_ready, out_copied = (sem("outc_done"), sem("ffn_scaled"), sem("x3_ready"),
                                                                   sem("outT_ready"), sem("out_copied"))

        A_GAMMA, A_BETA, A_ALPHA, F_GAMMA, F_BETA, F_ALPHA = range(6)

        def cvec(kind, b, c):
            return conds[:, kind, bass.ds(2 * b + c, 1)]

        LEAD, STEPS = 14, 4 * G

        def entries(step):
            units = range(0, LEAD) if step < 0 else range(LEAD + 2 * step, LEAD + 2 * step + 2)
            found = []
            for m in units:
                if m < 2 * NH:
                    found.append(("unit", m))
                if m >= 9 and (m - 9) % 8 == 0 and (m - 9) // 8 < G:
                    found.append(("turn", (m - 9) // 8))
            return found

        number = {}
        for s in range(-1, STEPS):
            for e in entries(s):
                number[e] = len(number)
        NENT = len(number)
        assert NENT == 2 * NH + G and NENT % 2 == 0
        BEFORE = [entries(-1)[i:i + 4] for i in range(0, len(entries(-1)), 4)]

        IN_ATT = {9: ["xT"], 11: ["down"], 12: ["up"], 14: ["sum"], 15: ["rows"]}
        for g in range(G - 1):
            IN_ATT.setdefault(4 * g + 5, []).append(f"den{g}")
            IN_ATT.setdefault(4 * g + 6, []).append(f"rec{g}")
        MID = ["q", "den3", "k", "rec3", "out_proj", "v", "back_sum", "back_rows", "ffn0", "ffn1", "ffn2", "ffn3",
               "before0", "ffn4", "before1", "ffn5", "before2", "ffn6", "before3", "ffn7", "ffn_out", "result"]
        FRONT = ["xT", "down", "up", "sum", "rows", "q", "k", "v", "before0", "before1", "before2", "before3"]

        def stages(names, front, back, b, more):
            for n in names:
                name, i = (n[:-1], int(n[-1])) if n[-1].isdigit() else (n, None)
                if name in front and more:
                    front[name](b + 1, False, *([] if i is None else [i]))
                if name in back:
                    back[name](b, *([] if i is None else [i]))

        def first_front(front):
            for n in FRONT:
                name, i = (n[:-1], int(n[-1])) if n[-1].isdigit() else (n, None)
                if name in front:
                    front[name](0, True, *([] if i is None else [i]))

        with nc.Block() as block:
            @block.sync
            def _(sp):
                def load(f, first):
                    if not first:
                        sp.wait_ge(xT_ready, 2 * f)
                        sp.sem_inc(passed_s, 1)
                        sp.wait_ge(adapter_w, 3 * f)
                        sp.sem_inc(passed_s, 1)
                    sp.dma_start(xnat[:], x[bass.ds(f, 1)].rearrange("b (t p) d -> p (b t) d", p=P)).then_inc(x_loaded, 16)
                    for m in range(2):
                        for e in range(2):
                            src = dw_scr[m, bass.ds(2 * f + e, 1)].rearrange("o c r n -> r (o c) n")
                            dst = dwl[e:P:2, m * D:(m + 1) * D].rearrange("p (c n) -> p c n", c=2)
                            sp.dma_start(dst, src).then_inc(dw_loaded, 16)

                def stacks(f, first):
                    for w in range(2):
                        sp.wait_ge(qk_b2, 4 * f + 2 * w + 2)
                        sp.dma_start(qk_scr[w].rearrange("t (c p) l -> p t c l", p=P), qks[:]).then_inc(parts_stored[w], 16)
                    if not first:
                        sp.wait_ge(score_ready, 64 * f)
                    for w, stack, parts in ((0, qst, Q_PARTS), (1, kst, K_PARTS)):
                        sp.wait_ge(parts_stored[w], 16 * f + 16)
                        for slot, part in enumerate(parts):
                            src = qk_scr[w, part].rearrange("(h d) l -> d h l", d=DH)
                            sp.dma_start(stack[DH * slot:DH * slot + DH], src).then_inc(stack_loaded, 16)

                def turns(b, found):
                    for kind, g in found:
                        if kind == "turn":
                            sp.wait_ge(neg_lo, G * b + g + 1)
                            for part in range(2):
                                row = KMAX + part
                                sp.dma_start(qst[row:row + 1, 4 * g:4 * g + 4, :], negrow[:, g, part, :]).then_inc(max_loaded[g % 2], 16)

                def body(b, more):
                    for s in range(STEPS):
                        turns(b, entries(s))
                    if more:
                        stacks(b + 1, False)
                        turns(b + 1, entries(-1))
                    sp.wait_ge(out_copied, 2 * b + 2)
                    sp.sem_inc(passed_s, 1)
                    sp.dma_start(out[bass.ds(b, 1)].rearrange("b (t p) d -> p (b t) d", p=P), onat[:]).then_inc(out_stored, 16)
                    sp.wait_ge(out_stored, 16 * b + 16)

                load(0, True)
                for row in (KMAX, KMAX + 1):
                    sp.dma_start(kst[row:row + 1, :, :], ones_bf[0:64, :]).then_inc(stack_ones, 16)
                sp.wait_ge(stack_ones, 32)
                stacks(0, True)
                turns(0, entries(-1))
                load(1, False)
                with sp.Fori(0, B - 2) as b:
                    body(b, True)
                    load(b + 2, False)
                body(B - 2, True)
                body(B - 1, False)

            @block.tensor
            def _(pe):
                def three_parts(out_, w, d, start, stop):
                    for i, (pw, pd) in enumerate(GATED_HI_LO):
                        mm = pe.matmul(out_, w(pw), d(pd), start=start and i == 0, stop=stop and i == 2)
                    return mm

                def s_xT(f, first):
                    pe.wait_ge(x_loaded, 16 * f + 16)
                    if not first:
                        pe.wait_ge(max_read, NENT * f)
                    for c in range(DC):
                        for t in range(NT):
                            mm = pe.transpose(ps[:, c, t * P:(t + 1) * P], xnat[:, t, c * P:(c + 1) * P], ident[:])
                        mm.then_inc(xT_ready, 1)

                def s_down(f, first):
                    pe.wait_ge(adapter_w, 3 * f + 3)
                    pe.wait_ge(x_hi, f + 1)
                    pe.wait_ge(x_lo, f + 1)
                    for c in range(DC):
                        mm = three_parts(ps[:, 2, :], lambda p: wa[:, p, c * P:(c + 1) * P], lambda p: xs[:, p, c, :],
                                         c == 0, c == DC - 1)
                    mm.then_inc(down_ready, 1)

                def s_up(f, first):
                    pe.wait_ge(down_hi, f + 1)
                    pe.wait_ge(down_lo, f + 1)
                    pe.wait_ge(xr_copied, DC * f + DC)
                    for m in range(DC):
                        three_parts(ps[:, m, :], lambda p: wa[:, p, D + m * P:D + (m + 1) * P], lambda p: dns[:, p, :],
                                    True, True).then_inc(up_ready, 1)

                def square_sums(bank, sq, ready):
                    for t in range(NT):
                        mm = pe.matmul(ps[:, bank, t:t + 1], sq[:, 0, t * P:(t + 1) * P], ones[:], start=True, stop=True)
                    mm.then_inc(ready, 1)

                def root_rows(bank, n, ready):
                    for t in range(NT):
                        mm = pe.transpose(ps[:, bank, t * P:(t + 1) * P], rst[:, n, 2, t:t + 1].broadcast_to([P, P]), ident[:])
                    mm.then_inc(ready, 1)

                def s_sum(f, first):
                    pe.wait_ge(x1_sqsum, f + 1)
                    square_sums(3, xn, sum_ready)

                def s_rows(f, first):
                    pe.wait_ge(rroot_step[0], 5 * f + 5)
                    root_rows(2, 0, x1_rows)

                def qk(w, f):
                    if w == 0:
                        pe.wait_ge(xn_hi, f + 1)
                        pe.wait_ge(xn_lo, f + 1)
                    for m in range(DC):
                        for c in range(DC):
                            mm = three_parts(ps[:, 2 * w + m, :], lambda p: wqk[:, w, p, c, m * P:(m + 1) * P],
                                             lambda p: xs[:, p, c, :], c == 0, c == DC - 1)
                        mm.then_inc(qk_ready[w], 1)

                def s_v(f, first):
                    pe.wait_ge(xn_ready, DC * f + DC)
                    pe.wait_ge(qk_copied, 4 * f + 2)
                    for t in range(NT):
                        for c in range(DC):
                            mm = pe.matmul(ps[:, t // 2, (t % 2) * D:(t % 2 + 1) * D], xn[:, c, t * P:(t + 1) * P], wv[:, c, :],
                                           start=(c == 0), stop=(c == DC - 1))
                        if t % 2:
                            mm.then_inc(v_ready, 1)

                def maxima(b, entry):
                    kind, m = entry
                    e = number[entry]
                    bank = 2 * (e % 2)
                    if e >= 2:
                        pe.wait_ge(max_read, NENT * b + e - 1)
                    if kind == "turn":
                        pe.wait_ge(max_read, NENT * b + number[("unit", 8 * m + 7)] + 1)
                        pe.transpose(ps[0:16, bank, 0:P], negmax[:, 4 * m:4 * m + 4, :].rearrange("p h t -> p (h t)"),
                                     ident[:]).then_inc(max_ready, 1)
                        return
                    for i in range(2):
                        t = 2 * (m % 2) + i
                        mm = pe.matmul(ps[:, bank + i, :], qst[0:KMAX, m // 2, t * P:(t + 1) * P], kst[0:KMAX, m // 2, :],
                                       start=True, stop=True)
                    mm.then_inc(max_ready, 1)

                def s_before(f, first, i):
                    if i == 0:
                        pe.wait_ge(stack_loaded, 192 * f + 192)
                        pe.wait_ge(qk_copied, 4 * f + 4)
                        pe.wait_ge(v_copied, 2 * f + 2)
                    for entry in BEFORE[i]:
                        maxima(f, entry)

                def score(b, s, j):
                    g, kt = divmod(s, 4)
                    if kt == 0 and j == 0:
                        pe.wait_ge(max_loaded[g % 2], 64 * b + 32 * (g // 2) + 32)
                    t = 4 * s + j
                    if t >= 2:
                        pe.wait_ge(exp_done, 64 * b + t - 1)
                    pe.matmul(ps[:, 4 + t % 2, :], kst[0:KALL, 4 * g + j, kt * P:(kt + 1) * P], qst[0:KALL, 4 * g + j, :],
                              start=True, stop=True).then_inc(score_ready, 1)

                def values(b, s):
                    g, kt = divmod(s, 4)
                    pe.wait_ge(exp_done, 64 * b + 4 * s + 4)
                    if kt == 0 and g >= 1:
                        pe.wait_ge(u_copied, G * b + g)
                    for j in range(4):
                        mm = pe.matmul(ps[32 * j:32 * j + 32, 7, :], vaug[:, kt, 4 * g + j, :], probs[:, s % NPR, j, :],
                                       start=(kt == 0), stop=(kt == 3), skip_group_check=True)
                    mm.then_inc(pv_done, 1)

                def s_den(b, g):
                    pe.wait_ge(u_copied, G * b + g + 1)
                    if g >= 1:
                        pe.wait_ge(o_scaled, G * b + g)
                    for t in range(NT):
                        mm = pe.transpose(ps[:, 6, t * P:(t + 1) * P], u[:, t * P:(t + 1) * P], ident[:])
                    mm.then_inc(den_ready, 1)

                def s_rec(b, g):
                    pe.wait_ge(rden_spread, G * b + g + 1)
                    for t in range(NT):
                        mm = pe.transpose(ps[:, 6, t * P:(t + 1) * P], rden_rows[:, t, :, :].rearrange("p j r -> p (j r)"), ident[:])
                    mm.then_inc(rec_ready, 1)

                def s_out_proj(b):
                    pe.wait_ge(o_scaled, G * b + G)
                    pe.wait_ge(o_hi, G * b + G)
                    pe.wait_ge(o_lo, G * b + G)
                    for m in range(DC):
                        for g in range(G):
                            mm = three_parts(ps[:, 6 + m, :], lambda p: wo[:, p, g, m * P:(m + 1) * P], lambda p: os_[:, p, g, :],
                                             g == 0, g == G - 1)
                        mm.then_inc(wo_ready, 1)

                def s_back_sum(b):
                    pe.wait_ge(x2_sqsum, b + 1)
                    square_sums(4, yn, x2_sum)

                def s_back_rows(b):
                    pe.wait_ge(rroot_step[1], 5 * b + 5)
                    root_rows(5, 1, x2_rows)

                def out_chunk(b, f):
                    pe.wait_ge(act_hi, FC * b + f + 1)
                    pe.wait_ge(act_lo, FC * b + f + 1)
                    for m in range(DC):
                        mm = three_parts(ps[:, 6 + m, :], lambda p: ow[:, p, f, m * P:(m + 1) * P], lambda p: acts[:, p, f % 2, :],
                                         f == 0, f == FC - 1)
                    mm.then_inc(outc_done, 1)

                def s_ffn(b, f):
                    if f == 0:
                        pe.wait_ge(y_hi, b + 1)
                        pe.wait_ge(y_lo, b + 1)
                    for w, bank, ready, read in ((gw, 4, gate_ready, silu_done), (hw, 5, hid_ready, act_ready)):
                        if f >= 1:
                            pe.wait_ge(read, FC * b + f)
                        for c in range(DC):
                            mm = three_parts(ps[:, bank, :], lambda p: w[:, p, c, f * P:(f + 1) * P], lambda p: ys[:, p, c, :],
                                             c == 0, c == DC - 1)
                        mm.then_inc(ready, 1)
                    if f >= 1:
                        out_chunk(b, f - 1)

                def s_result(b):
                    pe.wait_ge(x3_ready, DC * b + DC)
                    for t in range(NT):
                        for c in range(DC):
                            mm = pe.transpose(ps[:, 6 + t // 2, (t % 2) * D + c * P:(t % 2) * D + (c + 1) * P],
                                              xb[:, c, t * P:(t + 1) * P], ident[:])
                        if t % 2:
                            mm.then_inc(outT_ready, 1)
                    pe.wait_ge(out_copied, 2 * b + 2)

                front = {"xT": s_xT, "down": s_down, "up": s_up, "sum": s_sum, "rows": s_rows,
                         "q": lambda f, first: qk(0, f), "k": lambda f, first: qk(1, f), "v": s_v, "before": s_before}
                back = {"den": s_den, "rec": s_rec, "out_proj": s_out_proj, "back_sum": s_back_sum, "back_rows": s_back_rows,
                        "ffn": s_ffn, "ffn_out": lambda b: out_chunk(b, FC - 1), "result": s_result}

                def body(b, more):
                    for s in range(STEPS):
                        found = entries(s)
                        score(b, s, 0)
                        for entry in found[:1]:
                            maxima(b, entry)
                        score(b, s, 1)
                        if s >= 1:
                            values(b, s - 1)
                        score(b, s, 2)
                        for entry in found[1:]:
                            maxima(b, entry)
                        score(b, s, 3)
                        stages(IN_ATT.get(s, ()), front, back, b, more)
                    values(b, STEPS - 1)
                    stages(MID, front, back, b, more)

                first_front(front)
                with pe.Fori(0, B - 1) as b:
                    body(b, True)
                body(B - 1, False)

            @block.scalar
            def _(sc):
                def root(n, b):
                    sc.wait_ge(mean_ready[n], b + 1)
                    nc.scalar.activation(rst[:, n, 1, :], rst[:, n, 0, :], ACT.Sqrt).then_inc(root_ready[n], 1)

                def qk(w, f, first):
                    for m in range(DC):
                        sc.wait_ge(qk_ready[w], DC * f + m + 1)
                        if w == 1:
                            sc.wait_ge(qk_b2, 4 * f + m + 1)
                        elif not first:
                            sc.wait_ge(qk_b2, 4 * f)
                        nc.scalar.copy(qkf[:, m, :], ps[:, 2 * w + m, :]).then_inc(qk_copied, 1)

                def exps(b, s, j):
                    t = 4 * s + j
                    sc.wait_ge(score_ready, 64 * b + t + 1)
                    if j == 0 and s >= NPR:
                        sc.wait_ge(pv_done, STEPS * b + s - NPR + 1)
                    nc.scalar.activation(probs[:, s % NPR, j, :], ps[:, 4 + t % 2, :], ACT.Exp, scale=SCALE).then_inc(exp_done, 1)

                def u_copy(b, g):
                    sc.wait_ge(pv_done, STEPS * b + 4 * g + 4)
                    if g >= 1:
                        sc.wait_ge(o_lo, G * b + g)
                    nc.scalar.copy(u[:], ps[:, 7, :]).then_inc(u_copied, 1)

                def s_ffn(b, f):
                    sc.wait_ge(gate_ready, FC * b + f + 1)
                    if f >= 1:
                        sc.wait_ge(act_ready, FC * b + f)
                    nc.scalar.activation(sg[:], ps[:, 4, :], ACT.Silu).then_inc(silu_done, 1)

                def s_result(b):
                    for i in range(2):
                        sc.wait_ge(outT_ready, 2 * b + i + 1)
                        nc.scalar.copy(onat[:, 2 * i:2 * i + 2, :].rearrange("p t d -> p (t d)"), ps[:, 6 + i, :]).then_inc(out_copied, 1)

                front = {"sum": lambda f, first: root(0, f), "q": lambda f, first: qk(0, f, first),
                         "k": lambda f, first: qk(1, f, first)}
                back = {"back_sum": lambda b: root(1, b), "ffn": s_ffn, "result": s_result}

                def body(b, more):
                    for s in range(STEPS):
                        for j in range(4):
                            exps(b, s, j)
                            if j == 0 and s % 4 == 1 and s > 4:
                                u_copy(b, s // 4 - 1)
                        stages(IN_ATT.get(s, ()), front, back, b, more)
                    u_copy(b, G - 1)
                    stages(MID, front, back, b, more)

                first_front(front)
                with sc.Fori(0, B - 1) as b:
                    body(b, True)
                body(B - 1, False)

            @block.vector
            def _(dve):
                def s_xT(f, first):
                    if not first:
                        nc.vector.tensor_copy(xb[:], xr[:]).then_inc(x1_moved, 1)
                        dve.wait_ge(x1_moved, f)
                    for c in range(DC):
                        dve.wait_ge(xT_ready, DC * f + c + 1)
                        nc.vector.tensor_copy(xr[:, c, :], ps[:, c, :]).then_inc(xr_copied, 1)
                    dve.wait_ge(xr_copied, DC * f + DC)
                    nc.vector.tensor_copy(xs[:, 0], xr[:]).then_inc(x_hi, 1)
                    dve.wait_ge(x_hi, f + 1)
                    nc.vector.tensor_tensor(xs[:, 1], xr[:], xs[:, 0], ALU.subtract).then_inc(x_lo, 1)

                def s_last_xT(b):
                    nc.vector.tensor_copy(xb[:], xr[:]).then_inc(x1_moved, 1)

                def s_down(f, first):
                    dve.wait_ge(down_ready, f + 1)
                    nc.vector.tensor_scalar(dn[:], ps[:, 2, :], bdc[:, 0:1], 0.0, ALU.add, ALU.max).then_inc(down_act, 1)
                    dve.wait_ge(down_act, f + 1)
                    nc.vector.tensor_copy(dns[:, 0], dn[:]).then_inc(down_hi, 1)
                    dve.wait_ge(down_hi, f + 1)
                    nc.vector.tensor_tensor(dns[:, 1], dn[:], dns[:, 0], ALU.subtract).then_inc(down_lo, 1)

                def s_up(f, first):
                    for m in range(DC):
                        dve.wait_ge(up_ready, DC * f + m + 1)
                        nc.vector.scalar_tensor_tensor(xr[:, m, :], ps[:, m, :], buc[:, m:m + 1], xr[:, m, :],
                                                       ALU.add, ALU.add).then_inc(x1_ready, 1)
                    dve.wait_ge(x1_ready, DC * f + DC)
                    nc.vector.tensor_tensor(xn[:], xr[:], xr[:], ALU.mult).then_inc(x1_sq, 1)
                    dve.wait_ge(x1_sq, f + 1)
                    nc.vector.tensor_tensor(xn[:, 0, :], xn[:, 0, :], xn[:, 1, :], ALU.add).then_inc(x1_sqsum, 1)

                def rroot(n, b, bank, ready):
                    mean, rt, y = rst[:, n, 0, :], rst[:, n, 1, :], rst[:, n, 2, :]
                    t = nwt[:, n, :]
                    dve.wait_ge(ready, b + 1)
                    nc.vector.tensor_scalar(mean, ps[:, bank, 0:NT], 1.0 / D, EPS, ALU.mult, ALU.add).then_inc(mean_ready[n], 1)
                    dve.wait_ge(root_ready[n], b + 1)
                    nc.vector.reciprocal(y, rt).then_inc(rroot_step[n], 1)
                    dve.wait_ge(rroot_step[n], 5 * b + 1)
                    nc.vector.tensor_tensor(t, y, y, ALU.mult).then_inc(rroot_step[n], 1)
                    dve.wait_ge(rroot_step[n], 5 * b + 2)
                    nc.vector.tensor_tensor(t, t, mean, ALU.mult).then_inc(rroot_step[n], 1)
                    dve.wait_ge(rroot_step[n], 5 * b + 3)
                    nc.vector.tensor_scalar(t, t, -0.5, 1.5, ALU.mult, ALU.add).then_inc(rroot_step[n], 1)
                    dve.wait_ge(rroot_step[n], 5 * b + 4)
                    nc.vector.tensor_tensor(y, y, t, ALU.mult).then_inc(rroot_step[n], 1)

                def s_rows(f, first):
                    dve.wait_ge(x1_rows, f + 1)
                    for c in range(DC):
                        nc.vector.tensor_tensor(xn[:, c, :], xr[:, c, :], ps[:, 2, :], ALU.mult).then_inc(xn_scaled, 1)
                    for c in range(DC):
                        dve.wait_ge(xn_scaled, DC * f + c + 1)
                        nc.vector.tensor_scalar(xn[:, c, :], xn[:, c, :], cvec(A_GAMMA, f, c), cvec(A_BETA, f, c),
                                                ALU.mult, ALU.add).then_inc(xn_ready, 1)
                    dve.wait_ge(xn_ready, DC * f + DC)
                    nc.vector.tensor_copy(xs[:, 0], xn[:]).then_inc(xn_hi, 1)
                    dve.wait_ge(xn_hi, f + 1)
                    nc.vector.tensor_tensor(xs[:, 1], xn[:], xs[:, 0], ALU.subtract).then_inc(xn_lo, 1)

                def qk(w, f, first):
                    if w == 1:
                        dve.wait_ge(parts_stored[0], 16 * f + 16)
                    elif not first:
                        dve.wait_ge(parts_stored[1], 16 * f)
                    for m in range(DC):
                        dve.wait_ge(qk_copied, 4 * f + 2 * w + m + 1)
                        nc.vector.tensor_copy(qks[:, 0, m, :], qkf[:, m, :]).then_inc(qk_b0, 1)
                    for m in range(DC):
                        dve.wait_ge(qk_r1, 4 * f + 2 * w + m + 1)
                        nc.vector.tensor_copy(qks[:, 1, m, :], qkf[:, m, :]).then_inc(qk_b1, 1)

                def s_v(f, first):
                    for i in range(2):
                        dve.wait_ge(v_ready, 2 * f + i + 1)
                        nc.vector.tensor_copy(vaug[:, 2 * i:2 * i + 2, :, 0:DH],
                                              ps[:, i, :].rearrange("p (t h d) -> p t h d", t=2, h=NH)).then_inc(v_copied, 1)

                def maxima(b, entry):
                    kind, m = entry
                    e = number[entry]
                    bank = 2 * (e % 2)
                    dve.wait_ge(max_ready, NENT * b + e + 1)
                    if kind == "unit":
                        h, t = m // 2, 2 * (m % 2)
                        nc.vector.tensor_reduce(negmax[:, h, t:t + 2], ps[:, bank:bank + 2, :], AX_X, ALU.max,
                                                negate=True).then_inc(max_read, 1)
                        return
                    nc.vector.tensor_copy(negrow[:, m, 0, :], ps[0:16, bank, 0:P]).then_inc(neg_hi, 1)
                    dve.wait_ge(neg_hi, G * b + m + 1)
                    if m >= 1:
                        dve.wait_ge(neg_lo, G * b + m)
                    nc.vector.tensor_tensor(negrest[:], ps[0:16, bank, 0:P], negrow[:, m, 0, :], ALU.subtract).then_inc(max_read, 1)
                    dve.wait_ge(max_read, NENT * b + e + 1)
                    nc.vector.tensor_copy(negrow[:, m, 1, :], negrest[:]).then_inc(neg_lo, 1)

                def s_before(f, first, i):
                    for entry in BEFORE[i]:
                        maxima(f, entry)

                def s_den(b, g):
                    dve.wait_ge(den_ready, G * b + g + 1)
                    src = ps[:, 6, :].rearrange("p (t j r) -> p t j r", t=NT, j=4)[:, :, :, DH]
                    nc.vector.reciprocal(rden[:], src).then_inc(rden_ready, 1)
                    dve.wait_ge(rden_ready, G * b + g + 1)
                    nc.vector.tensor_copy(rden_rows[:], rden[:].unsqueeze(3).broadcast_to([P, NT, 4, 32])).then_inc(rden_spread, 1)

                def s_rec(b, g):
                    dve.wait_ge(rec_ready, G * b + g + 1)
                    nc.vector.tensor_tensor(u[:], u[:], ps[:, 6, :], ALU.mult).then_inc(o_scaled, 1)
                    dve.wait_ge(o_scaled, G * b + g + 1)
                    nc.vector.tensor_copy(os_[:, 0, g, :], u[:]).then_inc(o_hi, 1)

                def s_out_proj(b):
                    for m in range(DC):
                        dve.wait_ge(wo_ready, DC * b + m + 1)
                        if m == 0:
                            dve.wait_ge(x1_moved, b + 1)
                        nc.vector.scalar_tensor_tensor(xb[:, m, :], ps[:, 6 + m, :], cvec(A_ALPHA, b, m), xb[:, m, :],
                                                       ALU.mult, ALU.add).then_inc(x2_ready, 1)
                        dve.wait_ge(x2_ready, DC * b + m + 1)
                        nc.vector.tensor_tensor(yn[:, m, :], xb[:, m, :], xb[:, m, :], ALU.mult).then_inc(x2_sq, 1)
                    dve.wait_ge(x2_sq, DC * b + DC)
                    nc.vector.tensor_tensor(yn[:, 0, :], yn[:, 0, :], yn[:, 1, :], ALU.add).then_inc(x2_sqsum, 1)

                def s_back_rows(b):
                    dve.wait_ge(x2_rows, b + 1)
                    for c in range(DC):
                        nc.vector.tensor_tensor(yn[:, c, :], xb[:, c, :], ps[:, 5, :], ALU.mult).then_inc(yn_scaled, 1)
                    for c in range(DC):
                        dve.wait_ge(yn_scaled, DC * b + c + 1)
                        nc.vector.tensor_scalar(yn[:, c, :], yn[:, c, :], cvec(F_GAMMA, b, c), cvec(F_BETA, b, c),
                                                ALU.mult, ALU.add).then_inc(yn_ready, 1)
                    dve.wait_ge(yn_ready, DC * b + DC)
                    nc.vector.tensor_copy(ys[:, 0], yn[:]).then_inc(y_hi, 1)
                    dve.wait_ge(y_hi, b + 1)
                    nc.vector.tensor_tensor(ys[:, 1], yn[:], ys[:, 0], ALU.subtract).then_inc(y_lo, 1)

                def s_ffn(b, f):
                    dve.wait_ge(hid_ready, FC * b + f + 1)
                    dve.wait_ge(silu_done, FC * b + f + 1)
                    if f >= 2:
                        dve.wait_ge(outc_done, FC * b + f - 1)
                    nc.vector.tensor_tensor(act[:, f % 2, :], ps[:, 5, :], sg[:], ALU.mult).then_inc(act_ready, 1)
                    dve.wait_ge(act_ready, FC * b + f + 1)
                    nc.vector.tensor_copy(acts[:, 0, f % 2, :], act[:, f % 2, :]).then_inc(act_hi, 1)

                def s_ffn_out(b):
                    dve.wait_ge(outc_done, FC * b + FC)
                    for m in range(DC):
                        if m == 1:
                            dve.wait_ge(x3_ready, DC * b + 1)
                        nc.vector.tensor_scalar(tmp[:], ps[:, 6 + m, :], obc[:, m:m + 1], cvec(F_ALPHA, b, m),
                                                ALU.add, ALU.mult).then_inc(ffn_scaled, 1)
                        dve.wait_ge(ffn_scaled, DC * b + m + 1)
                        nc.vector.tensor_tensor(xb[:, m, :], xb[:, m, :], tmp[:], ALU.add).then_inc(x3_ready, 1)

                front = {"xT": s_xT, "down": s_down, "up": s_up, "sum": lambda f, first: rroot(0, f, 3, sum_ready),
                         "rows": s_rows, "q": lambda f, first: qk(0, f, first), "k": lambda f, first: qk(1, f, first),
                         "v": s_v, "before": s_before}
                back = {"den": s_den, "rec": s_rec, "out_proj": s_out_proj, "back_sum": lambda b: rroot(1, b, 4, x2_sum),
                        "back_rows": s_back_rows, "ffn": s_ffn, "ffn_out": s_ffn_out}

                def body(b, more):
                    for s in range(STEPS):
                        for entry in entries(s):
                            maxima(b, entry)
                        if not more and "xT" in IN_ATT.get(s, ()):
                            s_last_xT(b)
                        stages(IN_ATT.get(s, ()), front, back, b, more)
                    stages(MID, front, back, b, more)

                nc.vector.memset(vaug[:, :, :, DH:32], 1.0).then_inc(vones, 1)
                first_front(front)
                with dve.Fori(0, B - 1) as b:
                    body(b, True)
                body(B - 1, False)

            @block.gpsimd
            def _(pool):
                def s_xT(f, first):
                    pool.wait_ge(dw_loaded, 64 * f + 64)
                    nc.gpsimd.tensor_tensor(wa[:, 0], dwl[:], base[:], ALU.add).then_inc(adapter_w, 1)
                    pool.wait_ge(adapter_w, 3 * f + 1)
                    nc.gpsimd.tensor_tensor(dwl[:], dwl[:], base[:], ALU.add).then_inc(adapter_w, 1)
                    pool.wait_ge(adapter_w, 3 * f + 2)
                    nc.gpsimd.tensor_tensor(wa[:, 1], dwl[:], wa[:, 0], ALU.subtract).then_inc(adapter_w, 1)

                def qk(w, f):
                    for m in range(DC):
                        i = 4 * f + 2 * w + m + 1
                        pool.wait_ge(qk_b0, i)
                        nc.gpsimd.tensor_tensor(qkf[:, m, :], qkf[:, m, :], qks[:, 0, m, :], ALU.subtract).then_inc(qk_r1, 1)
                    for m in range(DC):
                        i = 4 * f + 2 * w + m + 1
                        pool.wait_ge(qk_b1, i)
                        nc.gpsimd.tensor_tensor(qks[:, 2, m, :], qkf[:, m, :], qks[:, 1, m, :], ALU.subtract).then_inc(qk_b2, 1)

                def s_rec(b, g):
                    pool.wait_ge(o_hi, G * b + g + 1)
                    nc.gpsimd.tensor_tensor(os_[:, 1, g, :], u[:], os_[:, 0, g, :], ALU.subtract).then_inc(o_lo, 1)

                def s_ffn(b, f):
                    pool.wait_ge(act_hi, FC * b + f + 1)
                    nc.gpsimd.tensor_tensor(acts[:, 1, f % 2, :], act[:, f % 2, :], acts[:, 0, f % 2, :],
                                            ALU.subtract).then_inc(act_lo, 1)

                front = {"xT": s_xT, "q": lambda f, first: qk(0, f), "k": lambda f, first: qk(1, f)}
                back = {"rec": s_rec, "ffn": s_ffn}

                def body(b, more):
                    for s in range(STEPS):
                        stages(IN_ATT.get(s, ()), front, back, b, more)
                    stages(MID, front, back, b, more)

                first_front(front)
                with pool.Fori(0, B - 1) as b:
                    body(b, True)
                body(B - 1, False)


_CONDS = ["L1_cond_attn_gamma_w", "L1_cond_attn_beta_w", "L1_cond_attn_alpha_w",
          "L1_cond_ffn_gamma_w", "L1_cond_ffn_beta_w", "L1_cond_ffn_alpha_w"]
_FIRST = ["x", "cond_256", "L0_cond_Wd", "L0_cond_bd", "L0_cond_Wu", "L0_cond_bu", "L0_cond_Wdd", "L0_cond_bdd",
          "L0_cond_Wdu", "L0_cond_bdu"]
_LAST = ["L1_cond_W_q", "L1_cond_W_k", "L1_cond_W_v", "L1_cond_W_o", "L1_cond_gate_w", "L1_cond_hidden_w",
         "L1_cond_out_w", "L1_cond_out_b"]


def kernel(**inputs):
    import concourse.bacc as bacc
    from concourse.bass_utils import run_bass_kernel_spmd

    nc = bacc.Bacc("TRN2", target_bir_lowering=False, num_devices=1)
    arrays = {}

    def given(name):
        a = np.ascontiguousarray(inputs[name])
        arrays[f"in_{name}"] = a
        return nc.dram_tensor(f"in_{name}", a.shape, mybir.dt.from_np(a.dtype), kind="ExternalInput").ap()

    first = [given(n) for n in _FIRST]
    conds = [given(n) for n in _CONDS]
    last = [given(n) for n in _LAST]
    out = nc.dram_tensor("out", inputs["x"].shape, F32, kind="ExternalOutput").ap()
    adapter_block_kernel(nc, *first, conds, *last, out)
    r = run_bass_kernel_spmd(nc, [arrays], core_ids=[0])
    return r.results[0]["out"]
```

```python
import numpy as np
import concourse.bass as bass
from concourse import mybir
from contextlib import ExitStack

F32, F32R, BF16, I32 = mybir.dt.float32, mybir.dt.float32r, mybir.dt.bfloat16, mybir.dt.int32
ALU = mybir.AluOpType
ACT = mybir.ActivationFunctionType
AX_X = mybir.AxisListType.X

P = 128
EPS = 1e-6
DELTA = 0.1


def adapter_block_kernel(nc, x, cond, Wd, bd, Wu, bu, Wdd, bdd, Wdu, bdu, cond_ws, Wq, Wk, Wv, Wo,
                         gate_w, hidden_w, out_w, out_b, out):
    B, L, D = x.shape
    BN = Wd.shape[0]
    HC = cond.shape[1]
    DH = 16
    NH = D // DH
    F = gate_w.shape[0]
    DC = D // P
    FC = F // P
    NT = L // P
    G = NH // 4
    HH = NH // DC
    SCALE = (NH / D) ** 0.5
    assert BN == P and HC == 64 and L == 512 and DC == 2 and NT == 4 and G == 4

    with ExitStack() as ctx:
        def sem(name):
            return ctx.enter_context(nc.semaphore(name))

        end_of = [16512]

        def place(name, shape, dt=F32, at=None):
            size = (2 if dt == BF16 else 4) * int(np.prod(shape[1:]))
            start = end_of[0] if at is None else at
            if at is None:
                end_of[0] = -(-(start + size) // 32) * 32
            assert start + size <= 229344, (name, start + size)
            return nc.alloc_sbuf_tensor_at(name, shape, dt, offset=start)

        ps = ctx.enter_context(nc.psum_tensor("ps", [P, 8, 512], F32))
        dw_scr = nc.dram_tensor("dw_scr", (2, 8, 2, 64, P), F32).ap()
        qk_scr = nc.dram_tensor("qk_scr", (2, 3, D, L), BF16).ap()

        ident = place("ident", [P, P])
        ones = place("ones", [P, 1])
        ones_bf = place("ones_bf", [P, P], BF16)
        bdc = place("bdc", [P, 1])
        buc = place("buc", [P, DC])
        obc = place("obc", [P, DC])
        gamma38 = place("gamma38", [P, 2 * B])
        aob = place("aob", [P, B, DC])
        conds = place("conds", [P, 6, 8])
        base = place("base", [P, 512])
        wqk = place("wqk", [P, 2, 2, DC, D], F32R)
        wv = place("wv", [P, DC, D])
        wo = place("wo", [P, 2, G, D], F32R)
        gw = place("gw", [P, 2, DC, F], F32R)
        hw = place("hw", [P, 2, DC, F], F32R)
        ow = place("ow", [P, 2, FC, D], F32R)
        xnat = place("xnat", [P, NT, D])
        xr = place("xr", [P, DC, L])
        xs = place("xs", [P, 2, DC, L], F32R)
        dwl = place("dwl", [P, 512])
        wa = place("wa", [P, 2, 512], F32R)
        NPR = 3
        probs_at = end_of[0]
        probs = place("probs", [P, NPR, 4, L])
        staged_at = end_of[0]
        Q_PARTS, K_PARTS = (0, 0, 1, 1, 0, 2), (0, 1, 0, 1, 2, 0)
        KMAX, KALL = 6 * DH, 6 * DH + 2
        kst = place("kst", [P, NH, L], BF16)
        qst = place("qst", [P, NH, L], BF16)
        vaug = place("vaug", [P, NT, NH, 32])
        dn_at = end_of[0]
        dn = place("dn", [P, L])
        dns = place("dns", [P, 2, L], F32R)
        xn = place("xn", [P, DC, L])
        qkf = [place("qf", [P, DC, L]), place("kf", [P, DC, L])]
        qks = [place("qs", [P, 3, DC, L], BF16), place("ks", [P, 3, DC, L], BF16, at=dn_at)]
        negmax = place("negmax", [P, NH, NT])
        negrow = place("negrow", [16, G, 2, P], BF16)
        negrest = place("negrest", [16, P])
        rst = place("rst", [P, 2, 2, NT])
        nwt = place("nwt", [P, 2, NT])
        rden = place("rden", [P, NT, 4])
        rden_rows = place("rden_rows", [P, NT, 4, 32])
        u = place("u", [P, L])
        xb = place("xb", [P, DC, L])
        os_at = end_of[0]
        os_ = place("os_", [P, 2, G, L], F32R)
        act = place("act", [P, 2, L], at=os_at)
        acts = place("acts", [P, 2, 2, L], F32R, at=os_at + 4096)
        onat = place("onat", [P, NT, D], at=os_at + 12288)
        ys = place("ys", [P, 2, DC, L], F32R, at=probs_at)
        yn = place("yn", [P, DC, L], at=probs_at + 8192)
        sg = place("sg", [P, L], at=probs_at + 12288)
        late_f = place("late_f", [P, 2, 512], at=os_at + 12288)

        gh_in = place("gh_in", [P, 2, FC, D], at=probs_at)
        ow_in = place("ow_in", [P, DC, F], at=probs_at + 16384)
        loop_end = end_of[0]
        end_of[0] = staged_at
        NST = 4
        dd_in = place("dd_in", [P, NST, 2048])
        qkvo_in = place("qkvo_in", [P, 4, DC, D])
        wo_pad = place("wo_pad", [P, DC, G, 4, 32])
        ddT = place("ddT", [P, 2, 4, 512])
        dw_out = place("dw_out", [P, 2, 4, 512])
        base_in = place("base_in", [P, 512])
        bias_in = place("bias_in", [P, 512])
        cw_in = place("cw_in", [P, 6, 2, HC])
        cwT = place("cwT", [P, 6, P])
        crows = place("crows", [32, P])
        csel = place("csel", [P, 32])
        end_of[0] = max(end_of[0], loop_end)

        groups = ["cond0", "cond1", "condm", "base", "v"]
        late = ["q", "k", "o0", "o1"] + [f"{w}{k}{half}" for w in "gh" for k in range(DC) for half in range(2)]
        late += [f"w{p}" for p in range(FC // 2)]
        loads_of = {"cond0": "cw", "cond1": "cw", "condm": "cond", "base": "base"}
        NCH = 16
        first_group = [-(-c * len(groups) // NCH) for c in range(NCH + 1)]

        dd_loaded = sem("dd_loaded")
        dd_loaded = [dd_loaded] + [sem(f"dd_loaded{i}") for i in range(1, NST)]
        w_loaded = {n: sem(f"w_loaded_{n}") for n in ("cond", "cw", "base", "v", "qko", "gate", "hidden", "outw", "vec")}
        const_ready = sem("const_ready")
        csel_turned, csel_ready = sem("csel_turned"), sem("csel_ready")
        base_summed = sem("base_summed")
        pad_ready = sem("pad_ready")
        ddT_ready = sem("ddT_ready")
        ddT_copied_a = sem("ddT_copied_a")
        ddT_copied_v = sem("ddT_copied_v")
        dw_ready = sem("dw_ready")
        dw_copied = sem("dw_copied")
        dw_stored = [sem("dw_stored0"), sem("dw_stored1")]
        dw_stored_last = sem("dw_stored_last")
        wt_ready = sem("wt_ready")
        late_ready, late_hi, late_read, late_lo = sem("late_ready"), sem("late_hi"), sem("late_read"), sem("late_lo")
        wt_hi = sem("wt_hi")
        wt_copied = sem("wt_copied")
        cwT_copied = sem("cwT_copied")

        def blocks_of(g):
            if g == "cond0":
                return [(cw_in[:, k, :, :].rearrange("p e h -> p (e h)"), k * P) for k in range(4)]
            if g == "cond1":
                return [(cw_in[:, k, :, :].rearrange("p e h -> p (e h)"), (k - 4) * P) for k in range(4, 6)]
            if g == "base":
                return [(base_in[:, i * P:(i + 1) * P], i * P) for i in range(4)]
            if g in "qkv":
                i = "qkv".index(g)
                return [(qkvo_in[:, i, m, k * P:(k + 1) * P], k * D + m * P) for k in range(DC) for m in range(DC)]
            if g[0] == "o":
                return [(wo_pad[:, m, 2 * int(g[1]) + i, :, :].rearrange("p j r -> p (j r)"), i * D + m * P)
                        for i in range(2) for m in range(DC)]
            if g[0] in "gh":
                w, k, half = "gh".index(g[0]), int(g[1]), int(g[2])
                return [(gh_in[:, w, 4 * half + i, k * P:(k + 1) * P], i * P) for i in range(4)]
            p = int(g[1])
            return [(ow_in[:, m, (2 * p + i) * P:(2 * p + i + 1) * P], i * D + m * P)
                    for i in range(2) for m in range(DC)]

        def kept_at(g, part):
            if g in "qk":
                return wqk[:, "qk".index(g), part, :, :].rearrange("p k n -> p (k n)")
            if g[0] == "o":
                i = 2 * int(g[1])
                return wo[:, part, i:i + 2, :].rearrange("p g n -> p (g n)")
            if g[0] in "gh":
                k, half = int(g[1]), int(g[2])
                return (gw if g[0] == "g" else hw)[:, part, k, half * 512:(half + 1) * 512]
            p = int(g[1])
            return ow[:, part, 2 * p:2 * p + 2, :].rearrange("p f n -> p (f n)")

        def load_name(g):
            if g in loads_of:
                return loads_of[g]
            return {"q": "qko", "k": "qko", "v": "v", "o": "qko", "g": "gate", "h": "hidden", "w": "outw"}[g[0]]

        x_loaded, dw_loaded = sem("x_loaded"), sem("dw_loaded")
        parts_stored = [sem("q_stored"), sem("k_stored")]
        stack_loaded = [sem("stack_loaded0"), sem("stack_loaded1")]
        max_loaded = [sem("max_loaded0"), sem("max_loaded1")]
        out_stored, stack_ones, vones, passed_s = sem("out_stored"), sem("stack_ones"), sem("vones"), sem("passed_s")
        xT_ready, down_ready, up_ready, sum_ready = sem("xT_ready"), sem("down_ready"), sem("up_ready"), sem("sum_ready")
        x1_rows, aob_ready = sem("x1_rows"), sem("aob_ready")
        qk_ready, v_ready = [sem("q_ready"), sem("k_ready")], sem("v_ready")
        xr_copied, x_hi, x_lo, adapter_w = sem("xr_copied"), sem("x_hi"), sem("x_lo"), sem("adapter_w")
        down_act, down_hi, down_lo = sem("down_act"), sem("down_hi"), sem("down_lo")
        x1_moved, x1_ready, x1_sq, x1_sqsum = sem("x1_moved"), sem("x1_ready"), sem("x1_sq"), sem("x1_sqsum")
        xn_scaled, xn_ready, xn_hi, xn_lo = sem("xn_scaled"), sem("xn_ready"), sem("xn_hi"), sem("xn_lo")
        qk_b0, qk_r1, qk_b1, qk_b2, v_copied = (sem("qk_b0"), sem("qk_r1"), sem("qk_b1"),
                                                           sem("qk_b2"), sem("v_copied"))
        rroot_step = [sem("x1_rroot"), sem("x2_rroot")]
        max_ready, max_read, neg_hi, neg_lo = (sem("max_ready"), sem("max_read"), sem("neg_hi"),
                                                         sem("neg_lo"))
        score_ready, exp_done, pv_done = sem("score_ready"), sem("exp_done"), sem("pv_done")
        rden_spread = sem("rden_spread")
        u_copied, den_ready, rden_ready, rec_ready, o_scaled, o_hi, o_lo = (
            sem("u_copied"), sem("den_ready"), sem("rden_ready"), sem("rec_ready"), sem("o_scaled"), sem("o_hi"), sem("o_lo"))
        wo_ready, x2_ready, x2_sq, x2_sum = sem("wo_ready"), sem("x2_ready"), sem("x2_sq"), sem("x2_sum")
        x2_rows, yn_scaled, y_hi, y_lo = sem("x2_rows"), sem("yn_scaled"), sem("y_hi"), sem("y_lo")
        gate_ready, hid_ready, silu_done, act_ready, act_hi, act_lo = (sem("gate_ready"), sem("hid_ready"), sem("silu_done"),
                                                                       sem("act_ready"), sem("act_hi"), sem("act_lo"))
        outc_done, ffn_ready, bias_added, x3_ready, outT_ready, out_copied = (sem("outc_done"), sem("ffn_ready"), sem("bias_added"), sem("x3_ready"),
                                                                   sem("outT_ready"), sem("out_copied"))

        A_GAMMA, A_BETA, A_ALPHA, F_GAMMA, F_BETA, F_ALPHA = range(6)

        def cvec(kind, b, c):
            return conds[:, kind, bass.ds(2 * b + c, 1)]

        LEAD, UNITS, STEPS = 30, 4, 4 * G

        def entries(step):
            units = range(0, LEAD) if step < 0 else range(LEAD + UNITS * step, LEAD + UNITS * step + UNITS)
            found = []
            for m in units:
                if m < NT * NH:
                    found.append(("unit", m))
                if m >= 17 and (m - 17) % 16 == 0 and (m - 17) // 16 < G:
                    found.append(("turn", (m - 17) // 16))
            return found

        number = {}
        for s in range(-1, STEPS):
            for e in entries(s):
                number[e] = len(number)
        NENT = len(number)
        assert NENT == NT * NH + G and NENT % 2 == 0
        NSOME = 2 * FC - 2
        FIRST_SOME = (2, 1, 1)
        cuts = [sum(FIRST_SOME[:i]) for i in range(len(FIRST_SOME))]
        cuts += [sum(FIRST_SOME) + (len(entries(-1)) - sum(FIRST_SOME)) * i // NSOME for i in range(NSOME + 1)]
        NBEF = len(cuts) - 1
        BEFORE = [entries(-1)[cuts[i]:cuts[i + 1]] for i in range(NBEF)]

        RROOT, C38 = 9, 3.0 / 8.0

        AHEAD = 2
        IN_ATT = {4: ["moved", "xT"], 5: ["xcopy"], 6: ["xsplit"], 8: ["down"], 9: ["relu"], 11: ["up"], 12: ["resid"],
                  13: ["squares"], 15: ["sum"], 16: ["rroot"], 18: ["rows"], 19: ["scale"], 20: ["affine"], 21: ["split"],
                  23: ["q"], 24: ["qsplit"], 25: ["k"], 27: ["ksplit"]}
        for g, halves in enumerate(((8, 9, 10, 12, 14), (16, 17, 18, 19, 20), (24, 25, 26, 27, 28))):
            for h, name in zip(halves, ("ucopy", "den", "recip", "rec", "oscale")):
                at = IN_ATT.setdefault(h, [])
                at.insert(1 if at == ["squares"] else 0, f"{name}{g}")
        MID = ["bank_left", "ucopy3", "outp0", "den3", "recip3", "outp1", "rec3", "oscale3", "outp2", "outp3", "va0", "va1",
               "xtwo", "vcopy0", "back_sum", "va2", "va3", "back_rows", "vcopy1", "back_low", "before0", "gate0", "before1",
               "hid0", "before2"]
        for f in range(1, FC):
            MID += [f"gate{f}", f"before{2 * f + 1}", f"hid{f}", f"before{2 * f + 2}"]
        MID += ["ffn_out", "step0", "result", "step1"]
        FRONT = ["xT", "xcopy", "xsplit", "late0", "late1", "late2", "late3", "down", "relu", "late4", "up", "resid", "squares",
                 "late5", "sum", "rroot", "late6", "rows", "scale", "affine", "split", "late7",
                 "q", "qsplit", "k", "ksplit", "va0", "va1", "va2", "va3", "vcopy0", "vcopy1", "late8", "late9", "late10", "late11"]
        TURNED = next(i for i in range(NBEF) if ("turn", 0) in BEFORE[i]) + 1
        FRONT += ["before0", "late12", "before1", "late13", "before2", "late14", "before3", "late15"]
        FRONT += [f"before{i}" for i in range(4, TURNED + 3)] + ["scores0"]
        FRONT += [f"before{i}" for i in range(TURNED + 3, NBEF)] + ["entries0", "scores1", "entries1"]

        def run_stage(n, table, *args):
            name = n.rstrip("0123456789")
            if name in table:
                table[name](*args, *([int(n[len(name):])] if n != name else []))

        def stages(names, front, back, b, more):
            for n in names:
                if more:
                    run_stage(n, front, b + 1, False)
                run_stage(n, back, b)

        def first_front(front):
            for n in FRONT:
                run_stage(n, front, 0, True)

        def dw_part(g, r):
            return dw_scr[r // 2, :, r % 2].rearrange("p (c g j) n -> g p c (j n)", c=4, g=4)[g]

        def adapter_weights(eng, ops, f):
            eng.wait_ge(dw_loaded, 64 * f + 64)
            ops.tensor_tensor(wa[:, 0], dwl[:], base[:], ALU.add).then_inc(adapter_w, 1)
            eng.wait_ge(adapter_w, 3 * f + 1)
            ops.tensor_tensor(dwl[:], dwl[:], base[:], ALU.add).then_inc(adapter_w, 1)
            eng.wait_ge(adapter_w, 3 * f + 2)
            ops.tensor_tensor(wa[:, 1], dwl[:], wa[:, 0], ALU.subtract).then_inc(adapter_w, 1)

        with nc.Block() as block:
            @block.sync
            def _(sp):
                def load_x(f):
                    sp.dma_start(xnat[:], x[bass.ds(f, 1)].rearrange("b (t p) d -> p (b t) d", p=P)).then_inc(x_loaded, 16)

                def load_dw(f):
                    for m in range(2):
                        for e in range(2):
                            src = dw_scr[m, bass.ds(2 * f + e, 1)].rearrange("o c r n -> r (o c) n")
                            dst = dwl[e:P:2, m * D:(m + 1) * D].rearrange("p (c n) -> p c n", c=2)
                            sp.dma_start(dst, src).then_inc(dw_loaded, 16)

                def load(f):
                    sp.wait_ge(xT_ready, 2 * f)
                    sp.sem_inc(passed_s, 1)
                    sp.wait_ge(adapter_w, 3 * f)
                    sp.sem_inc(passed_s, 1)
                    load_x(f)
                    load_dw(f)

                def stack(f, w, half):
                    st, parts = ((qst, Q_PARTS), (kst, K_PARTS))[w]
                    heads = slice(half * HH, half * HH + HH)
                    sp.wait_ge(parts_stored[w], 16 * f + 16)
                    for slot, part in enumerate(parts):
                        src = qk_scr[w, part, half * P:(half + 1) * P].rearrange("(h d) l -> d h l", d=DH)
                        sp.dma_start(st[DH * slot:DH * slot + DH, heads], src).then_inc(stack_loaded[half], 16)

                def stacks(f, first):
                    for w in range(2):
                        sp.wait_ge(qk_b2, 4 * f + 2 * w + 2)
                        sp.dma_start(qk_scr[w].rearrange("t (c p) l -> p t c l", p=P), qks[w][:]).then_inc(parts_stored[w], 16)
                    if not first:
                        sp.wait_ge(score_ready, 64 * f - 32)
                    stack(f, 0, 0)
                    stack(f, 1, 0)
                    if not first:
                        sp.wait_ge(score_ready, 64 * f)
                    stack(f, 0, 1)
                    stack(f, 1, 1)

                def turns(b, found):
                    for kind, g in found:
                        if kind == "turn":
                            sp.wait_ge(neg_lo, G * b + g + 1)
                            for part in range(2):
                                row = KMAX + part
                                sp.dma_start(qst[row:row + 1, 4 * g:4 * g + 4, :], negrow[:, g, part, :]).then_inc(max_loaded[g % 2], 16)

                def body(b, more, load_next):
                    for s in range(AHEAD, STEPS):
                        turns(b, entries(s))
                    if load_next:
                        load(b + 2)
                    if more:
                        stacks(b + 1, False)
                        for s in range(-1, AHEAD):
                            turns(b + 1, entries(s))
                    sp.wait_ge(out_copied, 2 * b + 2)
                    sp.sem_inc(passed_s, 1)
                    sp.dma_start(out[bass.ds(b, 1)].rearrange("b (t p) d -> p (b t) d", p=P), onat[:]).then_inc(out_stored, 16)
                    sp.wait_ge(out_stored, 16 * b + 16)
                    sp.sem_inc(passed_s, 1)

                def chunk(c):
                    if c >= NST:
                        sp.wait_ge(ddT_ready, 4 * (c - NST + 1))
                    if c < NCH // 2:
                        src = Wdd.rearrange("(n d) h -> n (d h)", d=D)[:, c * 2048:(c + 1) * 2048]
                    else:
                        dc, nb = divmod(c - NCH // 2, 4)
                        src = Wdu.rearrange("(dc dp n) h -> dc dp (n h)", dc=DC, n=BN)[dc][:, nb * 2048:(nb + 1) * 2048]
                    sp.dma_start(dd_in[:, c % NST], src).then_inc(dd_loaded[c % NST], 16)

                chunk(0)
                chunk(1)
                sp.wait_ge(const_ready, 1)
                for e in range(2):
                    sp.dma_start(crows[e:2 * B:2, e * HC:(e + 1) * HC], cond).then_inc(w_loaded["cond"], 16)
                chunk(2)
                for k, w in enumerate(cond_ws):
                    sp.dma_start(cw_in[:, k], w.rearrange("(e p) h -> p e h", p=P)).then_inc(w_loaded["cw"], 16)
                sp.dma_start(base_in[:, 0:D], Wd).then_inc(w_loaded["base"], 16)
                sp.dma_start(base_in[:, D:512], Wu.rearrange("(c p) n -> p c n", p=P)).then_inc(w_loaded["base"], 16)
                sp.dma_start(bias_in[:, 0:D], bdd.rearrange("(n d) -> n d", d=D)).then_inc(w_loaded["base"], 16)
                sp.dma_start(bias_in[:, D:512], bdu.rearrange("(c p n) -> p c n", p=P, n=BN)).then_inc(w_loaded["base"], 16)
                chunk(3)
                sp.dma_start(qkvo_in[:, 2], Wv.rearrange("(m p) k -> p m k", p=P)).then_inc(w_loaded["v"], 16)
                sp.dma_start(bdc[:], bd.rearrange("(p o) -> p o", o=1)).then_inc(w_loaded["vec"], 16)
                for c in range(DC):
                    for to, vec in ((buc, bu), (obc, out_b)):
                        src = vec[c * P:(c + 1) * P].rearrange("(p o) -> p o", o=1)
                        sp.dma_start(to[:, c:c + 1], src).then_inc(w_loaded["vec"], 16)
                for c in range(4, NCH):
                    chunk(c)
                load_x(0)
                for i, w in ((0, Wq), (1, Wk), (3, Wo)):
                    sp.dma_start(qkvo_in[:, i], w.rearrange("(m p) k -> p m k", p=P)).then_inc(w_loaded["qko"], 16)
                sp.wait_ge(dw_copied, NCH)
                for g in range(4):
                    sp.dma_start(dw_part(g, 3), dw_out[32 * g:32 * g + 8, 1]).then_inc(dw_stored_last, 16)
                sp.wait_ge(dw_stored[0], 128)
                sp.wait_ge(dw_stored[1], 64)
                sp.wait_ge(dw_stored_last, 64)
                load_dw(0)
                for row in (KMAX, KMAX + 1):
                    sp.dma_start(kst[row:row + 1, :, :], ones_bf[0:64, :]).then_inc(stack_ones, 16)
                sp.wait_ge(stack_ones, 32)
                sp.dma_start(gh_in[:, 0], gate_w.rearrange("(f p) k -> p f k", p=P)).then_inc(w_loaded["gate"], 16)
                sp.dma_start(gh_in[:, 1], hidden_w.rearrange("(f p) k -> p f k", p=P)).then_inc(w_loaded["hidden"], 16)
                sp.dma_start(ow_in[:], out_w.rearrange("(m p) f -> p m f", p=P)).then_inc(w_loaded["outw"], 16)
                stacks(0, True)
                load(1)
                for s in range(-1, AHEAD):
                    turns(0, entries(s))
                with sp.Fori(0, B - 2) as b:
                    body(b, True, True)
                body(B - 2, True, False)
                body(B - 1, False, False)

            @block.tensor
            def _(pe):
                def dd_transposes(c):
                    pe.wait_ge(dd_loaded[c % NST], 16 * (c // NST + 1))
                    for t in range(4):
                        if c >= 1:
                            pe.wait_ge(ddT_copied_v if t < 2 else ddT_copied_a, 2 * (c - 1) + t % 2 + 1)
                        for i in range(4):
                            j = 4 * t + i
                            mm = pe.transpose(ps[:, t, i * P:(i + 1) * P], dd_in[:, c % NST, j * P:(j + 1) * P], ident[:])
                        mm.then_inc(ddT_ready, 1)

                def dd_products(c):
                    if c == 0:
                        pe.wait_ge(csel_ready, 1)
                    pe.wait_ge(ddT_copied_v, 2 * (c + 1))
                    pe.wait_ge(ddT_copied_a, 2 * (c + 1))
                    if c >= 2:
                        pe.wait_ge(dw_copied, c - 1)
                    for t in range(4):
                        mm = pe.matmul(ps[32 * t:32 * t + 32, 4 + c % 2, :], csel[:], ddT[:, c % 2, t, :], start=True, stop=True)
                    mm.then_inc(dw_ready, 1)

                def weights(i):
                    g = groups[i]
                    if g == "condm":
                        pe.wait_ge(csel_ready, 1)
                        pe.wait_ge(cwT_copied, 2)
                        if i >= 2:
                            pe.wait_ge(wt_copied, i - 1)
                        for k in range(6):
                            mm = pe.matmul(ps[:, 6 + i % 2, 32 * k:32 * k + 32], cwT[:, k, :], csel[:], start=True, stop=True)
                        mm.then_inc(wt_ready, 1)
                        return
                    if g == "base":
                        pe.wait_ge(base_summed, 2)
                    else:
                        pe.wait_ge(w_loaded[load_name(g)], {"cw": 96}.get(load_name(g), 16))
                    if i >= 2:
                        pe.wait_ge(wt_copied, i - 1)
                    for src, col in blocks_of(g):
                        mm = pe.transpose(ps[:, 6 + i % 2, col:col + P], src, ident[:])
                    mm.then_inc(wt_ready, 1)

                pe.wait_ge(const_ready, 5)
                pe.wait_ge(w_loaded["cond"], 32)
                pe.transpose(ps[:, 4, 0:32], crows[:], ident[0:32, 0:32]).then_inc(csel_turned, 1)
                for c in range(NCH):
                    dd_transposes(c)
                    for i in range(first_group[c], first_group[c + 1]):
                        weights(i)
                    if c >= 1:
                        dd_products(c - 1)
                dd_products(NCH - 1)
                pe.wait_ge(wt_copied, len(groups))

                def s_late(f, first, i):
                    if late[i][0] == "o":
                        pe.wait_ge(pad_ready, 1 + DC)
                    else:
                        pe.wait_ge(w_loaded[load_name(late[i])], 48 if late[i] in "qk" else 16)
                    if i >= 2:
                        pe.wait_ge(late_read, i - 1)
                    for src, col in blocks_of(late[i]):
                        mm = pe.transpose(ps[:, 6 + i % 2, col:col + P], src, ident[:])
                    mm.then_inc(late_ready, 1)

                def s_xT(f, first):
                    pe.wait_ge(x_loaded, 16 * f + 16)
                    for c in range(DC):
                        for t in range(NT):
                            mm = pe.transpose(ps[:, 2 + c, t * P:(t + 1) * P], xnat[:, t, c * P:(c + 1) * P], ident[:])
                        mm.then_inc(xT_ready, 1)

                def s_down(f, first):
                    pe.wait_ge(adapter_w, 3 * f + 3)
                    pe.wait_ge(x_hi, f + 1)
                    for c in range(DC):
                        for pw in range(2):
                            pe.matmul(ps[:, 2, :], wa[:, pw, c * P:(c + 1) * P], xs[:, 0, c, :],
                                      start=(c == 0 and pw == 0), stop=False)
                    pe.wait_ge(x_lo, f + 1)
                    for c in range(DC):
                        mm = pe.matmul(ps[:, 2, :], wa[:, 0, c * P:(c + 1) * P], xs[:, 1, c, :], start=False, stop=(c == DC - 1))
                    mm.then_inc(down_ready, 1)

                def s_up(f, first):
                    pe.wait_ge(down_hi, f + 1)
                    for m in range(DC):
                        for pw in range(2):
                            pe.matmul(ps[:, 2 + m, :], wa[:, pw, D + m * P:D + (m + 1) * P], dns[:, 0, :], start=(pw == 0), stop=False)
                    pe.wait_ge(down_lo, f + 1)
                    for m in range(DC):
                        pe.matmul(ps[:, 2 + m, :], wa[:, 0, D + m * P:D + (m + 1) * P], dns[:, 1, :],
                                  start=False, stop=True).then_inc(up_ready, 1)

                def square_sums(bank, sq, added, b, ready):
                    pe.wait_ge(added, b + 1)
                    for t in range(NT):
                        mm = pe.matmul(ps[:, bank, t:t + 1], sq[:, 0, t * P:(t + 1) * P], ones[:], start=True, stop=True)
                    mm.then_inc(ready, 1)

                def root_rows(bank, n, ready):
                    for t in range(NT):
                        mm = pe.transpose(ps[:, bank, t * P:(t + 1) * P], rst[:, n, 1, t:t + 1].broadcast_to([P, P]), ident[:])
                    mm.then_inc(ready, 1)

                def s_sum(f, first):
                    square_sums(2, xn, x1_sqsum, f, sum_ready)

                def s_rows(f, first):
                    pe.wait_ge(rroot_step[0], RROOT * f + RROOT)
                    root_rows(3, 0, x1_rows)

                def qk(w, f, first):
                    if w == 1 and not first:
                        pe.wait_ge(max_read, NENT * f)
                    for m in range(DC):
                        bank = 2 * (1 - w) + m
                        for c in range(DC):
                            if w == 0 and m == 0:
                                pe.wait_ge(xn_hi, DC * f + c + 1)
                            for pw in range(2):
                                pe.matmul(ps[:, bank, :], wqk[:, w, pw, c, m * P:(m + 1) * P], xs[:, 0, c, :],
                                          start=(c == 0 and pw == 0), stop=False)
                        for c in range(DC):
                            if w == 0 and m == 0:
                                pe.wait_ge(xn_lo, DC * f + c + 1)
                            mm = pe.matmul(ps[:, bank, :], wqk[:, w, 0, c, m * P:(m + 1) * P], xs[:, 1, c, :],
                                           start=False, stop=(c == DC - 1))
                        mm.then_inc(qk_ready[w], 1)

                def s_va(f, first, i):
                    if i == 0:
                        pe.wait_ge(xn_ready, DC * f + DC)
                    for c in range(DC):
                        mm = pe.matmul(ps[:, 4 + i // 2, (i % 2) * D:(i % 2 + 1) * D], xn[:, c, i * P:(i + 1) * P], wv[:, c, :],
                                       start=(c == 0), stop=(c == DC - 1))
                    if i % 2:
                        mm.then_inc(v_ready, 1)

                def maxima(b, entry):
                    kind, m = entry
                    e = number[entry]
                    bank = e % 2
                    if e >= 2:
                        pe.wait_ge(max_read, NENT * b + e - 1)
                    if kind == "turn":
                        pe.wait_ge(max_read, NENT * b + number[("unit", 16 * m + 15)] + 1)
                        pe.transpose(ps[0:16, bank, 0:P], negmax[:, 4 * m:4 * m + 4, :].rearrange("p h t -> p (h t)"),
                                     ident[:]).then_inc(max_ready, 1)
                        return
                    h, t = divmod(m, NT)
                    if h % HH == 0 and t == 0:
                        pe.wait_ge(stack_loaded[h // HH], 192 * b + 192)
                    pe.matmul(ps[:, bank, :], qst[0:KMAX, h, t * P:(t + 1) * P], kst[0:KMAX, h, :],
                              start=True, stop=True).then_inc(max_ready, 1)

                def s_before(f, first, i):
                    for entry in BEFORE[i]:
                        maxima(f, entry)

                def score(b, s, j):
                    g, kt = divmod(s, 4)
                    if kt == 0 and j == 0:
                        pe.wait_ge(max_loaded[g % 2], 64 * b + 32 * (g // 2) + 32)
                    t = 4 * s + j
                    if t >= 2:
                        pe.wait_ge(exp_done, 64 * b + t - 1)
                    pe.matmul(ps[:, 4 + t % 2, :], kst[0:KALL, 4 * g + j, kt * P:(kt + 1) * P], qst[0:KALL, 4 * g + j, :],
                              start=True, stop=True).then_inc(score_ready, 1)

                def values(b, s):
                    g, kt = divmod(s, 4)
                    pe.wait_ge(exp_done, 64 * b + 4 * s + 4)
                    if kt == 0 and g >= 1:
                        pe.wait_ge(u_copied, G * b + g)
                    for j in range(4):
                        mm = pe.matmul(ps[32 * j:32 * j + 32, 7, :], vaug[:, kt, 4 * g + j, :], probs[:, s % NPR, j, :],
                                       start=(kt == 0), stop=(kt == 3), skip_group_check=True)
                    mm.then_inc(pv_done, 1)

                def s_den(b, g):
                    pe.wait_ge(u_copied, G * b + g + 1)
                    if g >= 1:
                        pe.wait_ge(o_scaled, G * b + g)
                    for t in range(NT):
                        mm = pe.transpose(ps[:, 6, t * P:(t + 1) * P], u[:, t * P:(t + 1) * P], ident[:])
                    mm.then_inc(den_ready, 1)

                def s_rec(b, g):
                    pe.wait_ge(rden_spread, G * b + g + 1)
                    for t in range(NT):
                        mm = pe.transpose(ps[:, 6, t * P:(t + 1) * P], rden_rows[:, t, :, :].rearrange("p j r -> p (j r)"), ident[:])
                    mm.then_inc(rec_ready, 1)

                def s_outp(b, g):
                    pe.wait_ge(o_hi, G * b + g + 1)
                    if g == G - 1:
                        for m in range(DC):
                            for pw, pd in ((0, 0), (1, 0), (0, 1)):
                                if m == 0 and pd == 1:
                                    pe.wait_ge(o_lo, G * b + g + 1)
                                mm = pe.matmul(ps[:, 2 + m, :], wo[:, pw, g, m * P:(m + 1) * P], os_[:, pd, g, :],
                                               start=False, stop=(pd == 1))
                            mm.then_inc(wo_ready, 1)
                        return
                    for m in range(DC):
                        for pw in range(2):
                            pe.matmul(ps[:, 2 + m, :], wo[:, pw, g, m * P:(m + 1) * P], os_[:, 0, g, :],
                                      start=(g == 0 and pw == 0), stop=False)
                    pe.wait_ge(o_lo, G * b + g + 1)
                    for m in range(DC):
                        mm = pe.matmul(ps[:, 2 + m, :], wo[:, 0, g, m * P:(m + 1) * P], os_[:, 1, g, :],
                                       start=False, stop=False)

                def s_back_sum(b):
                    pe.wait_ge(x2_sq, DC * b + DC)
                    for t in range(NT):
                        for c in range(DC):
                            mm = pe.matmul(ps[:, 6, t:t + 1], yn[:, c, t * P:(t + 1) * P], ones[:], start=(c == 0), stop=(c == DC - 1))
                    mm.then_inc(x2_sum, 1)

                def s_back_rows(b):
                    pe.wait_ge(rroot_step[1], RROOT * b + RROOT)
                    root_rows(7, 1, x2_rows)

                def out_chunk(b, f):
                    pe.wait_ge(act_hi, FC * b + f + 1)
                    for m in range(DC):
                        for pw in range(2):
                            pe.matmul(ps[:, 6 + m, :], ow[:, pw, f, m * P:(m + 1) * P], acts[:, 0, f % 2, :],
                                      start=(f == 0 and pw == 0), stop=False)
                    pe.wait_ge(act_lo, FC * b + f + 1)
                    for m in range(DC):
                        mm = pe.matmul(ps[:, 6 + m, :], ow[:, 0, f, m * P:(m + 1) * P], acts[:, 1, f % 2, :],
                                       start=False, stop=(f == FC - 1))
                        if f == FC - 1:
                            mm.then_inc(ffn_ready, 1)
                    if f < FC - 1:
                        mm.then_inc(outc_done, 1)

                def ffn_in(b, f, w, bank, ready, read):
                    if f >= 1:
                        pe.wait_ge(read, FC * b + f)
                    for c in range(DC):
                        if f == 0:
                            pe.wait_ge(y_hi, DC * b + c + 1)
                        for pw in range(2):
                            pe.matmul(ps[:, bank, :], w[:, pw, c, f * P:(f + 1) * P], ys[:, 0, c, :],
                                      start=(c == 0 and pw == 0), stop=False)
                    for c in range(DC):
                        if f == 0:
                            pe.wait_ge(y_lo, DC * b + c + 1)
                        mm = pe.matmul(ps[:, bank, :], w[:, 0, c, f * P:(f + 1) * P], ys[:, 1, c, :],
                                       start=False, stop=(c == DC - 1))
                    mm.then_inc(ready, 1)

                def s_gate(b, f):
                    ffn_in(b, f, gw, 4, gate_ready, silu_done)

                def s_hid(b, f):
                    ffn_in(b, f, hw, 5, hid_ready, act_ready)
                    if f >= 1:
                        out_chunk(b, f - 1)

                def s_result(b):
                    pe.wait_ge(x3_ready, DC * b + DC)
                    for t in range(NT):
                        for c in range(DC):
                            mm = pe.transpose(ps[:, 2 + t // 2, (t % 2) * D + c * P:(t % 2) * D + (c + 1) * P],
                                              xb[:, c, t * P:(t + 1) * P], ident[:])
                        if t % 2:
                            mm.then_inc(outT_ready, 1)

                def step(b, s, at_half=lambda h: None, found=None):
                    found = entries(s) if found is None else found
                    for j in range(4):
                        score(b, s, j)
                        for entry in found[j:j + 1] if j < 3 else found[3:]:
                            maxima(b, entry)
                        if j == 1 and s >= 1:
                            values(b, s - 1)
                        if j % 2:
                            at_half(2 * s + j // 2)

                front = {"bank_left": lambda f, first: pe.wait_ge(qk_r1, 4 * f + 2),
                         "late": s_late, "xT": s_xT, "down": s_down, "up": s_up, "sum": s_sum, "rows": s_rows,
                         "q": lambda f, first: qk(0, f, first), "k": lambda f, first: qk(1, f, first), "va": s_va, "before": s_before,
                         "step": lambda f, first, s: step(f, s), "scores": lambda f, first, s: step(f, s, found=()),
                         "entries": lambda f, first, s: [maxima(f, entry) for entry in entries(s)]}
                back = {"den": s_den, "rec": s_rec, "outp": s_outp, "back_sum": s_back_sum, "back_rows": s_back_rows,
                        "gate": s_gate, "hid": s_hid, "ffn_out": lambda b: out_chunk(b, FC - 1), "result": s_result}

                def body(b, more):
                    for s in range(AHEAD, STEPS):
                        step(b, s, lambda h: stages(IN_ATT.get(h, ()), front, back, b, more))
                    values(b, STEPS - 1)
                    stages(MID, front, back, b, more)
                    pe.wait_ge(out_copied, 2 * b + 2)

                first_front(front)
                pe.wait_ge(late_lo, len(late))
                with pe.Fori(0, B - 1) as b:
                    body(b, True)
                body(B - 1, False)

            @block.scalar
            def _(sc):
                for c in range(NCH + 1):
                    if c < NCH:
                        if c >= 2:
                            sc.wait_ge(dw_ready, c - 1)
                        for t in (2, 3):
                            sc.wait_ge(ddT_ready, 4 * c + t + 1)
                            nc.scalar.copy(ddT[:, c % 2, t, :], ps[:, t, :]).then_inc(ddT_copied_a, 1)
                    if c >= 1:
                        sc.wait_ge(dw_ready, c)
                        if c > 8:
                            sc.wait_ge(dw_stored[(c - 1) // 4 % 2], 64)
                        nc.scalar.mul(dw_out[:, (c - 1) // 4 % 2, (c - 1) % 4, :], ps[:, 4 + (c - 1) % 2, :], DELTA).then_inc(dw_copied, 1)

                def s_late(f, first, i):
                    sc.wait_ge(late_ready, i + 1)
                    nc.scalar.copy(kept_at(late[i], 0), ps[:, 6 + i % 2, :]).then_inc(late_hi, 1)
                    if i >= 2:
                        sc.wait_ge(late_lo, i - 1)
                    nc.scalar.copy(late_f[:, i % 2, :], ps[:, 6 + i % 2, :]).then_inc(late_read, 1)

                def squares(sq, x_, made, b, ready):
                    for c in range(DC):
                        sc.wait_ge(made, DC * b + c + 1)
                        nc.scalar.activation(sq[:, c, :], x_[:, c, :], ACT.Square).then_inc(ready, 1)

                def s_back_rows(b):
                    for c in range(DC):
                        sc.wait_ge(yn_scaled, DC * b + c + 1)
                        nc.scalar.activation(ys[:, 0, c, :], yn[:, c, :], ACT.Identity, bias=cvec(F_BETA, b, c)).then_inc(y_hi, 1)

                def exps(b, s, j):
                    t = 4 * s + j
                    sc.wait_ge(score_ready, 64 * b + t + 1)
                    if j == 0 and s >= NPR:
                        sc.wait_ge(pv_done, STEPS * b + s - NPR + 1)
                    nc.scalar.activation(probs[:, s % NPR, j, :], ps[:, 4 + t % 2, :], ACT.Exp, scale=SCALE).then_inc(exp_done, 1)

                def u_copy(b, g):
                    sc.wait_ge(pv_done, STEPS * b + 4 * g + 4)
                    if g >= 1:
                        sc.wait_ge(o_lo, G * b + g)
                    nc.scalar.copy(u[:], ps[:, 7, :]).then_inc(u_copied, 1)

                def s_gate(b, f):
                    sc.wait_ge(gate_ready, FC * b + f + 1)
                    if f >= 1:
                        sc.wait_ge(act_ready, FC * b + f)
                    nc.scalar.activation(sg[:], ps[:, 4, :], ACT.Silu).then_inc(silu_done, 1)

                def s_hid(b, f):
                    if f == 1:
                        sc.wait_ge(yn_scaled, DC * b + DC)
                        sc.wait_ge(aob_ready, 1 + DC)
                        for c in range(DC):
                            nc.scalar.activation(xb[:, c, :], xb[:, c, :], ACT.Identity, bias=aob[:, bass.ds(b, 1), c]).then_inc(bias_added, 1)

                def s_xcopy(f, first):
                    for c in range(DC):
                        sc.wait_ge(xT_ready, DC * f + c + 1)
                        nc.scalar.copy(xr[:, c, :], ps[:, 2 + c, :]).then_inc(xr_copied, 1)

                def s_relu(f, first):
                    sc.wait_ge(down_ready, f + 1)
                    nc.scalar.activation(dn[:], ps[:, 2, :], ACT.Relu, bias=bdc[:, 0:1]).then_inc(down_act, 1)

                def s_moved(b):
                    nc.scalar.copy(xb[:], xr[:]).then_inc(x1_moved, 1)
                    sc.wait_ge(x1_moved, b + 1)

                def s_result(b):
                    for i in range(2):
                        sc.wait_ge(outT_ready, 2 * b + i + 1)
                        nc.scalar.copy(onat[:, 2 * i:2 * i + 2, :].rearrange("p t d -> p (t d)"), ps[:, 2 + i, :]).then_inc(out_copied, 1)

                def step(b, s, at_half=lambda h: None):
                    for j in range(4):
                        exps(b, s, j)
                        if j == 2 and s == 4:
                            u_copy(b, 0)
                        if j % 2:
                            at_half(2 * s + j // 2)

                front = {"late": s_late, "xcopy": s_xcopy, "relu": s_relu, "squares": lambda f, first: squares(xn, xr, x1_ready, f, x1_sq),
                         "step": lambda f, first, s: step(f, s), "scores": lambda f, first, s: step(f, s)}
                back = {"moved": s_moved, "xtwo": lambda b: squares(yn, xb, x2_ready, b, x2_sq),
                        "gate": s_gate, "hid": s_hid, "result": s_result,
                        "back_rows": s_back_rows, "ucopy": lambda b, g: u_copy(b, g) if g == G - 1 else None}

                def body(b, more):
                    for s in range(AHEAD, STEPS):
                        step(b, s, lambda h: stages(IN_ATT.get(h, ()), front, back, b, more))
                    stages(MID, front, back, b, more)

                first_front(front)
                with sc.Fori(0, B - 1) as b:
                    body(b, True)
                body(B - 1, False)

            @block.vector
            def _(dve):
                def copy_weights(i):
                    g, bank = groups[i], 6 + i % 2
                    dve.wait_ge(wt_ready, i + 1)
                    if g == "cond0":
                        nc.vector.tensor_copy(cwT[:, 0:4, :].rearrange("p k n -> p (k n)"), ps[:, bank, :]).then_inc(cwT_copied, 1)
                        dve.wait_ge(cwT_copied, 1)
                        nc.vector.engine_nop().then_inc(wt_copied, 1)
                    elif g == "cond1":
                        nc.vector.tensor_copy(cwT[:, 4:6, :].rearrange("p k n -> p (k n)"), ps[:, bank, 0:2 * P]).then_inc(cwT_copied, 1)
                        dve.wait_ge(cwT_copied, 2)
                        nc.vector.engine_nop().then_inc(wt_copied, 1)
                    elif g == "condm":
                        src = ps[:, bank, 0:192].rearrange("p (k n) -> p k n", k=6)[:, :, 0:8]
                        nc.vector.tensor_copy(conds[:], src).then_inc(wt_copied, 1)
                    elif g == "base":
                        nc.vector.tensor_copy(base[:], ps[:, bank, :]).then_inc(wt_copied, 1)
                    elif g == "v":
                        nc.vector.tensor_copy(wv[:].rearrange("p k n -> p (k n)"), ps[:, bank, :]).then_inc(wt_copied, 1)
                    else:
                        nc.vector.tensor_copy(kept_at(g, 0), ps[:, bank, :]).then_inc(wt_hi, 1)
                        his[0] += 1
                        dve.wait_ge(wt_hi, his[0])
                        nc.vector.tensor_tensor(kept_at(g, 1), ps[:, bank, :], kept_at(g, 0), ALU.subtract).then_inc(wt_copied, 1)

                his = [0]
                dve.wait_ge(csel_turned, 1)
                nc.vector.tensor_copy(csel[:], ps[:, 4, 0:32]).then_inc(csel_ready, 1)
                for c in range(NCH):
                    if c >= 2:
                        dve.wait_ge(dw_ready, c - 1)
                    for t in (0, 1):
                        dve.wait_ge(ddT_ready, 4 * c + t + 1)
                        nc.vector.tensor_copy(ddT[:, c % 2, t, :], ps[:, t, :]).then_inc(ddT_copied_v, 1)
                    for i in range(first_group[c], first_group[c + 1]):
                        copy_weights(i)
                dve.wait_ge(w_loaded["vec"], 80)

                def s_xsplit(f, first):
                    dve.wait_ge(xr_copied, DC * f + DC)
                    nc.vector.tensor_copy(xs[:, 0], xr[:]).then_inc(x_hi, 1)
                    if first:
                        dve.wait_ge(x_hi, f + 1)
                        nc.vector.tensor_tensor(xs[:, 1], xr[:], xs[:, 0], ALU.subtract).then_inc(x_lo, 1)
                        adapter_weights(dve, nc.vector, f)

                def s_relu(f, first):
                    if first:
                        dve.wait_ge(down_ready, f + 1)
                        nc.vector.memset(vaug[:, :, :, DH:32], 1.0).then_inc(vones, 1)
                    dve.wait_ge(down_act, f + 1)
                    nc.vector.tensor_copy(dns[:, 0], dn[:]).then_inc(down_hi, 1)
                    if first:
                        dve.wait_ge(down_hi, f + 1)
                        nc.vector.tensor_tensor(dns[:, 1], dn[:], dns[:, 0], ALU.subtract).then_inc(down_lo, 1)

                def s_resid(f, first):
                    for m in range(DC):
                        dve.wait_ge(up_ready, DC * f + m + 1)
                        nc.vector.scalar_tensor_tensor(xr[:, m, :], ps[:, 2 + m, :], buc[:, m:m + 1], xr[:, m, :],
                                                       ALU.add, ALU.add).then_inc(x1_ready, 1)

                def rroot(n, b, bank, ready):
                    mean, y, t = rst[:, n, 0, :], rst[:, n, 1, :], nwt[:, n, :]
                    steps = (lambda: nc.vector.tensor_scalar(mean, ps[:, bank, 0:NT], 1.0 / D, EPS, ALU.mult, ALU.add),
                             lambda: nc.vector.tensor_scalar(y.bitcast(I32), mean.bitcast(I32), -0.5, float(0x5F3759DF),
                                                             ALU.mult, ALU.add),
                             lambda: nc.vector.tensor_tensor(t, y, y, ALU.mult),
                             lambda: nc.vector.tensor_tensor(t, t, mean, ALU.mult),
                             lambda: nc.vector.scalar_tensor_tensor(t, t, -10.0 / 3.0, t, ALU.add, ALU.mult),
                             lambda: nc.vector.scalar_tensor_tensor(y, t, 5.0, y, ALU.add, ALU.mult),
                             lambda: nc.vector.tensor_tensor(t, y, y, ALU.mult),
                             lambda: nc.vector.scalar_tensor_tensor(t, t, -0.5 * C38 ** 2, mean, ALU.mult, ALU.mult),
                             lambda: nc.vector.scalar_tensor_tensor(y, t, 1.5, y, ALU.add, ALU.mult))
                    dve.wait_ge(ready, b + 1)
                    for i, one in enumerate(steps):
                        if i:
                            dve.wait_ge(rroot_step[n], RROOT * b + i)
                        one().then_inc(rroot_step[n], 1)

                def scale_rows(y, x_, bank, rows, scaled, b):
                    dve.wait_ge(rows, b + 1)
                    for c in range(DC):
                        nc.vector.scalar_tensor_tensor(y[:, c, :], x_[:, c, :], C38, ps[:, bank, :], ALU.mult, ALU.mult).then_inc(scaled, 1)

                def split(y, yh, ready, hi, b, lo=None):
                    for c in range(DC):
                        dve.wait_ge(ready, DC * b + c + 1)
                        nc.vector.tensor_copy(yh[:, 0, c, :], y[:, c, :]).then_inc(hi, 1)
                        if lo is not None:
                            dve.wait_ge(hi, DC * b + c + 1)
                            nc.vector.tensor_tensor(yh[:, 1, c, :], y[:, c, :], yh[:, 0, c, :], ALU.subtract).then_inc(lo, 1)

                def qk(w, f, first):
                    rest, part = qkf[w], qks[w]
                    if not first:
                        dve.wait_ge(parts_stored[w], 16 * f)
                    for m in range(DC):
                        i = 4 * f + 2 * w + m + 1
                        dve.wait_ge(qk_ready[w], DC * f + m + 1)
                        nc.vector.tensor_copy(part[:, 0, m, :], ps[:, 2 * (1 - w) + m, :]).then_inc(qk_b0, 1)
                        dve.wait_ge(qk_b0, i)
                        nc.vector.tensor_tensor(rest[:, m, :], ps[:, 2 * (1 - w) + m, :], part[:, 0, m, :], ALU.subtract).then_inc(qk_r1, 1)
                        dve.wait_ge(qk_r1, i)
                        nc.vector.tensor_copy(part[:, 1, m, :], rest[:, m, :]).then_inc(qk_b1, 1)
                        dve.wait_ge(qk_b1, i)
                        nc.vector.tensor_tensor(part[:, 2, m, :], rest[:, m, :], part[:, 1, m, :], ALU.subtract).then_inc(qk_b2, 1)

                def s_vcopy(f, first, i):
                    dve.wait_ge(v_ready, 2 * f + i + 1)
                    nc.vector.tensor_copy(vaug[:, 2 * i:2 * i + 2, :, 0:DH],
                                          ps[:, 4 + i, :].rearrange("p (t h d) -> p t h d", t=2, h=NH)).then_inc(v_copied, 1)

                def maxima(b, entry):
                    kind, m = entry
                    e = number[entry]
                    bank = e % 2
                    dve.wait_ge(max_ready, NENT * b + e + 1)
                    if kind == "unit":
                        h, t = divmod(m, NT)
                        nc.vector.tensor_reduce(negmax[:, h, t:t + 1], ps[:, bank, :], AX_X, ALU.max, negate=True).then_inc(max_read, 1)
                        return
                    nc.vector.tensor_copy(negrow[:, m, 0, :], ps[0:16, bank, 0:P]).then_inc(neg_hi, 1)
                    dve.wait_ge(neg_hi, G * b + m + 1)
                    if m >= 1:
                        dve.wait_ge(neg_lo, G * b + m)
                    nc.vector.tensor_tensor(negrest[:], ps[0:16, bank, 0:P], negrow[:, m, 0, :], ALU.subtract).then_inc(max_read, 1)
                    dve.wait_ge(max_read, NENT * b + e + 1)
                    nc.vector.tensor_copy(negrow[:, m, 1, :], negrest[:]).then_inc(neg_lo, 1)

                def s_before(f, first, i):
                    for entry in BEFORE[i]:
                        maxima(f, entry)

                def s_recip(b, g):
                    dve.wait_ge(den_ready, G * b + g + 1)
                    src = ps[:, 6, :].rearrange("p (t j r) -> p t j r", t=NT, j=4)[:, :, :, DH]
                    nc.vector.reciprocal(rden[:], src).then_inc(rden_ready, 1)
                    dve.wait_ge(rden_ready, G * b + g + 1)
                    nc.vector.tensor_copy(rden_rows[:], rden[:].unsqueeze(3).broadcast_to([P, NT, 4, 32])).then_inc(rden_spread, 1)

                def s_oscale(b, g):
                    dve.wait_ge(rec_ready, G * b + g + 1)
                    nc.vector.tensor_tensor(u[:], u[:], ps[:, 6, :], ALU.mult).then_inc(o_scaled, 1)
                    dve.wait_ge(o_scaled, G * b + g + 1)
                    nc.vector.tensor_copy(os_[:, 0, g, :], u[:]).then_inc(o_hi, 1)
                    if g == G - 1:
                        dve.wait_ge(o_hi, G * b + g + 1)
                        nc.vector.tensor_tensor(os_[:, 1, g, :], u[:], os_[:, 0, g, :], ALU.subtract).then_inc(o_lo, 1)

                def s_xtwo(b):
                    for m in range(DC):
                        dve.wait_ge(wo_ready, DC * b + m + 1)
                        if m == 0:
                            dve.wait_ge(x1_moved, b + 1)
                        nc.vector.scalar_tensor_tensor(xb[:, m, :], ps[:, 2 + m, :], cvec(A_ALPHA, b, m), xb[:, m, :],
                                                       ALU.mult, ALU.add).then_inc(x2_ready, 1)

                def s_back_rows(b):
                    dve.wait_ge(x2_ready, DC * b + DC)
                    dve.wait_ge(x2_rows, b + 1)
                    for c in range(DC):
                        nc.vector.scalar_tensor_tensor(yn[:, c, :], xb[:, c, :], gamma38[:, bass.ds(2 * b + c, 1)], ps[:, 7, :],
                                                       ALU.mult, ALU.mult).then_inc(yn_scaled, 1)

                def s_back_low(b):
                    for c in range(DC):
                        dve.wait_ge(y_hi, DC * b + c + 1)
                        nc.vector.scalar_tensor_tensor(ys[:, 1, c, :], yn[:, c, :], cvec(F_BETA, b, c), ys[:, 0, c, :],
                                                       ALU.add, ALU.subtract).then_inc(y_lo, 1)

                def s_ucopy(b, g):
                    if g in (0, G - 1):
                        return
                    dve.wait_ge(pv_done, STEPS * b + 4 * g + 4)
                    dve.wait_ge(o_lo, G * b + g)
                    nc.vector.tensor_copy(u[:], ps[:, 7, :]).then_inc(u_copied, 1)

                def s_affine(f, first):
                    for c in range(DC):
                        dve.wait_ge(xn_scaled, DC * f + c + 1)
                        nc.vector.tensor_scalar(xn[:, c, :], xn[:, c, :], cvec(A_GAMMA, f, c), cvec(A_BETA, f, c),
                                                ALU.mult, ALU.add).then_inc(xn_ready, 1)

                def s_hid(b, f):
                    dve.wait_ge(hid_ready, FC * b + f + 1)
                    dve.wait_ge(silu_done, FC * b + f + 1)
                    if f >= 2:
                        dve.wait_ge(outc_done, (FC - 1) * b + f - 1)
                    nc.vector.tensor_tensor(act[:, f % 2, :], ps[:, 5, :], sg[:], ALU.mult).then_inc(act_ready, 1)
                    dve.wait_ge(act_ready, FC * b + f + 1)
                    nc.vector.tensor_copy(acts[:, 0, f % 2, :], act[:, f % 2, :]).then_inc(act_hi, 1)

                def s_ffn_out(b):
                    for m in range(DC):
                        dve.wait_ge(ffn_ready, DC * b + m + 1)
                        dve.wait_ge(bias_added, DC * b + m + 1)
                        nc.vector.scalar_tensor_tensor(xb[:, m, :], ps[:, 6 + m, :], cvec(F_ALPHA, b, m), xb[:, m, :],
                                                       ALU.mult, ALU.add).then_inc(x3_ready, 1)

                def step(b, s, at_half=lambda h: None):
                    found = entries(s)
                    for half, some in enumerate((found[:2], found[2:])):
                        for entry in some:
                            maxima(b, entry)
                        at_half(2 * s + half)

                front = {"xsplit": s_xsplit, "relu": s_relu, "resid": s_resid, "rroot": lambda f, first: rroot(0, f, 2, sum_ready),
                         "scale": lambda f, first: scale_rows(xn, xr, 3, x1_rows, xn_scaled, f),
                         "split": lambda f, first: split(xn, xs, xn_ready, xn_hi, f, xn_lo if first else None),
                         "qsplit": lambda f, first: qk(0, f, first), "ksplit": lambda f, first: qk(1, f, first),
                         "affine": s_affine, "vcopy": s_vcopy, "before": s_before, "step": lambda f, first, s: step(f, s),
                         "entries": lambda f, first, s: [maxima(f, entry) for entry in entries(s)]}
                back = {"ucopy": s_ucopy, "recip": s_recip, "oscale": s_oscale, "xtwo": s_xtwo, "back_sum": lambda b: rroot(1, b, 6, x2_sum),
                        "back_rows": s_back_rows, "back_low": s_back_low, "hid": s_hid, "ffn_out": s_ffn_out}

                def body(b, more):
                    for s in range(AHEAD, STEPS):
                        step(b, s, lambda h: stages(IN_ATT.get(h, ()), front, back, b, more))
                    stages(MID, front, back, b, more)

                nc.vector.tensor_scalar(gamma38[:], conds[:, F_GAMMA, :], C38, None, ALU.mult).then_inc(aob_ready, 1)
                for c in range(DC):
                    alpha = conds[:, F_ALPHA, :].rearrange("p (b c) -> p b c", c=DC)[:, :, c]
                    nc.vector.tensor_scalar(aob[:, :, c], alpha, obc[:, c:c + 1], None, ALU.mult).then_inc(aob_ready, 1)
                first_front(front)
                with dve.Fori(0, B - 1) as b:
                    body(b, True)
                body(B - 1, False)

            @block.gpsimd
            def _(pool):
                nc.gpsimd.memset(crows[:], 0.0).then_inc(const_ready, 1)
                nc.gpsimd.memset(ident[:], 0.0).then_inc(const_ready, 1)
                nc.gpsimd.memset(ones[:], 1.0).then_inc(const_ready, 1)
                nc.gpsimd.memset(ones_bf[:], 1.0).then_inc(const_ready, 1)
                pool.wait_ge(const_ready, 4)
                nc.gpsimd.affine_select(out=ident[:], in_=ident[:], compare_op=ALU.not_equal, fill=1.0, base=0,
                                        pattern=[[-1, P]], channel_multiplier=1).then_inc(const_ready, 1)
                nc.gpsimd.memset(wo_pad[:], 0.0).then_inc(pad_ready, 1)
                pool.wait_ge(w_loaded["base"], 64)
                nc.gpsimd.tensor_scalar(bias_in[:], bias_in[:], DELTA, None, ALU.mult).then_inc(base_summed, 1)
                pool.wait_ge(base_summed, 1)
                nc.gpsimd.tensor_tensor(base_in[:], base_in[:], bias_in[:], ALU.add).then_inc(base_summed, 1)
                for r in range(3):
                    pool.wait_ge(dw_copied, 4 * (r + 1))
                    for g in range(4):
                        pool.dma_start(dw_part(g, r), dw_out[32 * g:32 * g + 8, r % 2]).then_inc(dw_stored[r % 2], 16)

                pool.wait_ge(w_loaded["qko"], 48)
                pool.wait_ge(pad_ready, 1)
                for m in range(DC):
                    nc.gpsimd.tensor_copy(wo_pad[:, m, :, :, 0:DH],
                                          qkvo_in[:, 3, m, :].rearrange("p (g j r) -> p g j r", g=G, j=4)).then_inc(pad_ready, 1)

                def s_late(f, first, i):
                    pool.wait_ge(late_hi, i + 1)
                    pool.wait_ge(late_read, i + 1)
                    nc.gpsimd.tensor_tensor(kept_at(late[i], 1), late_f[:, i % 2, :], kept_at(late[i], 0), ALU.subtract).then_inc(late_lo, 1)

                def s_xT(f, first):
                    if first:
                        return
                    adapter_weights(pool, nc.gpsimd, f)

                def low(y, yh, hi, lo, n, b):
                    for c in range(n):
                        pool.wait_ge(hi, n * b + c + 1)
                        nc.gpsimd.tensor_tensor(yh[:, 1, c, :], y[:, c, :], yh[:, 0, c, :], ALU.subtract).then_inc(lo, 1)

                def s_xsplit(f, first):
                    if first:
                        return
                    pool.wait_ge(x_hi, f + 1)
                    nc.gpsimd.tensor_tensor(xs[:, 1], xr[:], xs[:, 0], ALU.subtract).then_inc(x_lo, 1)

                def s_relu(f, first):
                    if first:
                        return
                    pool.wait_ge(down_hi, f + 1)
                    nc.gpsimd.tensor_tensor(dns[:, 1], dn[:], dns[:, 0], ALU.subtract).then_inc(down_lo, 1)

                def s_squares(f, first):
                    pool.wait_ge(x1_sq, DC * f + DC)
                    nc.gpsimd.tensor_tensor(xn[:, 0, :], xn[:, 0, :], xn[:, 1, :], ALU.add).then_inc(x1_sqsum, 1)

                def s_oscale(b, g):
                    if g == G - 1:
                        return
                    pool.wait_ge(o_hi, G * b + g + 1)
                    nc.gpsimd.tensor_tensor(os_[:, 1, g, :], u[:], os_[:, 0, g, :], ALU.subtract).then_inc(o_lo, 1)

                def s_hid(b, f):
                    pool.wait_ge(act_hi, FC * b + f + 1)
                    nc.gpsimd.tensor_tensor(acts[:, 1, f % 2, :], act[:, f % 2, :], acts[:, 0, f % 2, :],
                                            ALU.subtract).then_inc(act_lo, 1)

                front = {"late": s_late, "xT": s_xT, "xsplit": s_xsplit, "relu": s_relu, "squares": s_squares,
                         "split": lambda f, first: None if first else low(xn, xs, xn_hi, xn_lo, DC, f)}
                back = {"oscale": s_oscale, "hid": s_hid}

                def body(b, more):
                    for h in range(2 * AHEAD, 2 * STEPS):
                        stages(IN_ATT.get(h, ()), front, back, b, more)
                    stages(MID, front, back, b, more)

                first_front(front)
                with pool.Fori(0, B - 1) as b:
                    body(b, True)
                body(B - 1, False)


_CONDS = ["L1_cond_attn_gamma_w", "L1_cond_attn_beta_w", "L1_cond_attn_alpha_w",
          "L1_cond_ffn_gamma_w", "L1_cond_ffn_beta_w", "L1_cond_ffn_alpha_w"]
_FIRST = ["x", "cond_256", "L0_cond_Wd", "L0_cond_bd", "L0_cond_Wu", "L0_cond_bu", "L0_cond_Wdd", "L0_cond_bdd",
          "L0_cond_Wdu", "L0_cond_bdu"]
_LAST = ["L1_cond_W_q", "L1_cond_W_k", "L1_cond_W_v", "L1_cond_W_o", "L1_cond_gate_w", "L1_cond_hidden_w",
         "L1_cond_out_w", "L1_cond_out_b"]


def kernel(**inputs):
    import concourse.bacc as bacc
    from concourse.bass_utils import run_bass_kernel_spmd

    nc = bacc.Bacc("TRN2", target_bir_lowering=False, num_devices=1)
    arrays = {}

    def given(name):
        a = np.ascontiguousarray(inputs[name])
        arrays[f"in_{name}"] = a
        return nc.dram_tensor(f"in_{name}", a.shape, mybir.dt.from_np(a.dtype), kind="ExternalInput").ap()

    first = [given(n) for n in _FIRST]
    conds = [given(n) for n in _CONDS]
    last = [given(n) for n in _LAST]
    out = nc.dram_tensor("out", inputs["x"].shape, F32, kind="ExternalOutput").ap()
    adapter_block_kernel(nc, *first, conds, *last, out)
    r = run_bass_kernel_spmd(nc, [arrays], core_ids=[0])
    return r.results[0]["out"]
```
